# Optimizing a Trainium2 kernel written in Bass

```python
import numpy as np
import jax
import jax.numpy as jnp

def _softmax(x, axis=-1):
    return jax.nn.softmax(x, axis=axis)

def _gelu(x):
    return jax.nn.gelu(x, approximate=True)

def _silu(x):
    return jax.nn.silu(x)

def _sigmoid(x):
    return jax.nn.sigmoid(x)

def _layernorm(x, axis=-1, eps=1e-05):
    m = jnp.mean(x, axis=axis, keepdims=True)
    v = jnp.var(x, axis=axis, keepdims=True)
    return (x - m) / jnp.sqrt(v + eps)

def _scatter_add(tgt, idx, src, axis=0):
    return tgt.at[idx].add(src)

def _segment_sum(src, seg, n):
    return jax.ops.segment_sum(src, seg, n)
kernel_name = 'mk_xattn_ffn_d1_seqx_r8_c1ec95'

def setup_inputs(seed: int=0):
    np.random.seed(seed)
    _w = jnp.asarray

    def _rec_inputs():
        import jax
        import jax.numpy as jnp
        _rk = jax.random.key(seed)
        x = 7.22e-05 + 1 * jax.random.normal(jax.random.fold_in(_rk, 1), (32, 64, 256), jnp.float32)
        _lenS = 64 - jax.random.randint(jax.random.fold_in(_rk, 7), (32,), 0, max(1, 64 // 4) + 1, jnp.int32)
        _lenS2 = 64 - jax.random.randint(jax.random.fold_in(_rk, 8), (32,), 0, max(1, 64 // 4) + 1, jnp.int32)
        _ctx_1024P = jax.random.normal(jax.random.fold_in(_rk, 11), (32, 16, 128), jnp.float32)
        _ctx_1024c = jax.random.dirichlet(jax.random.fold_in(_rk, 511), 0.3 * jnp.ones((16,), jnp.float32), (32, 64))
        _ctx_1024t = jnp.einsum('bsk,bkd->bsd', _ctx_1024c, _ctx_1024P)
        _ctx_1024t = _ctx_1024t * jax.lax.rsqrt(jnp.mean(jnp.square(_ctx_1024t)) + 1e-12) * 0.953939
        ctx_1024 = -1.39393e-06 + 0.999914 * (_ctx_1024t + 0.3 * jax.random.normal(jax.random.fold_in(_rk, 611), (32, 64, 128), jnp.float32))
        fside_BxSx2_0 = jax.random.uniform(jax.random.fold_in(_rk, 12), (32, 64, 2), jnp.float32, 0.0, 0.999707)
        return (x, ctx_1024, fside_BxSx2_0)
    x, ctx_1024, fside_BxSx2_0 = _rec_inputs()

    def _L0_xattn_setup():
        import jax, jax.numpy as jnp
        import numpy as np
        DIM = 256
        CTX_DIM = 128
        N_HEADS = 32
        HEAD_DIM = DIM // N_HEADS
        POS_DIM = 2
        B, N, CTXN = (2, 256, 256)
        ROPE_BASE = 10000.0

        def apply_axial_rope(x, pos):
            b, n, h, d = x.shape
            p = pos.shape[-1]
            dpa = d // p
            half = dpa // 2
            freqs = ROPE_BASE ** (-jnp.arange(half, dtype=x.dtype) / half)
            ang = pos[..., :, None] * freqs
            cos = jnp.cos(ang)[:, :, None, :, :]
            sin = jnp.sin(ang)[:, :, None, :, :]
            xr = x.reshape(b, n, h, p, half, 2)
            x1, x2 = (xr[..., 0], xr[..., 1])
            out = jnp.stack([x1 * cos - x2 * sin, x1 * sin + x2 * cos], axis=-1)
            return out.reshape(b, n, h, d)
        key = jax.random.key(seed)
        ks = jax.random.split(key, 8)
        x = jax.random.normal(ks[0], (B, N, DIM), jnp.float32)
        ctx = jax.random.normal(ks[1], (B, CTXN, CTX_DIM), jnp.float32)
        pos_map = jax.random.uniform(ks[2], (B, N, POS_DIM), jnp.float32)
        ctx_pos_map = jax.random.uniform(ks[3], (B, CTXN, POS_DIM), jnp.float32)
        Wq = jax.random.normal(ks[4], (DIM, DIM), jnp.float32) / np.sqrt(DIM)
        Wkv = jax.random.normal(ks[5], (CTX_DIM, 2 * DIM), jnp.float32) / np.sqrt(CTX_DIM)
        Wout = jax.random.normal(ks[6], (DIM, DIM), jnp.float32) / np.sqrt(DIM)
        bout = jnp.zeros((DIM,), jnp.float32)
        return {'x': x, 'ctx': ctx, 'pos_map': pos_map, 'ctx_pos_map': ctx_pos_map, 'Wq': Wq, 'Wkv': Wkv, 'Wout': Wout, 'bout': bout}
    _L0_xattn_all = _L0_xattn_setup()
    _L0_xattn_in = {k: v for k, v in _L0_xattn_all.items() if k in ('Wq', 'Wkv', 'Wout', 'bout')}
    del _L0_xattn_all

    def _L0_ffn_setup():
        import jax, jax.numpy as jnp
        import numpy as np
        K_SKIP = 4
        NORM_TOPK = True
        key = jax.random.key(seed)
        k1, k2, k3, k4 = jax.random.split(key, 4)
        B, S, H, I, E = (1, 128, 256, 96, 64)
        hidden_states = jax.random.normal(k1, (B, S, H), dtype=jnp.float32)
        gate_weight = jax.random.normal(k2, (E, H), dtype=jnp.float32) * 0.02
        gate_up_proj = jax.random.normal(k3, (E, 2 * I, H), dtype=jnp.float32) * 0.02
        down_proj = jax.random.normal(k4, (E, H, I), dtype=jnp.float32) * 0.02
        return {'hidden_states': hidden_states, 'gate_weight': gate_weight, 'gate_up_proj': gate_up_proj, 'down_proj': down_proj}
    _L0_ffn_all = _L0_ffn_setup()
    _L0_ffn_in = {k: v for k, v in _L0_ffn_all.items() if k in ('gate_weight', 'gate_up_proj', 'down_proj')}
    del _L0_ffn_all
    return {'x': x, 'ctx_1024': ctx_1024, 'fside_BxSx2_0': fside_BxSx2_0, 'L0_xattn_Wq': _L0_xattn_in['Wq'], 'L0_xattn_Wkv': _L0_xattn_in['Wkv'], 'L0_xattn_Wout': _L0_xattn_in['Wout'], 'L0_xattn_bout': _L0_xattn_in['bout'], 'L0_ffn_gate_weight': _L0_ffn_in['gate_weight'], 'L0_ffn_gate_up_proj': _L0_ffn_in['gate_up_proj'], 'L0_ffn_down_proj': _L0_ffn_in['down_proj']}

def reference(x, ctx_1024, fside_BxSx2_0, L0_xattn_Wq, L0_xattn_Wkv, L0_xattn_Wout, L0_xattn_bout, L0_ffn_gate_weight, L0_ffn_gate_up_proj, L0_ffn_down_proj):
    import jax
    import jax.numpy as jnp

    def _L0_xattn_ref(x, ctx, pos_map, ctx_pos_map, Wq, Wkv, Wout, bout):
        import jax, jax.numpy as jnp
        import numpy as np
        DIM = 256
        CTX_DIM = 128
        N_HEADS = 32
        HEAD_DIM = DIM // N_HEADS
        POS_DIM = 2
        B, N, CTXN = (2, 256, 256)
        ROPE_BASE = 10000.0

        def apply_axial_rope(x, pos):
            b, n, h, d = x.shape
            p = pos.shape[-1]
            dpa = d // p
            half = dpa // 2
            freqs = ROPE_BASE ** (-jnp.arange(half, dtype=x.dtype) / half)
            ang = pos[..., :, None] * freqs
            cos = jnp.cos(ang)[:, :, None, :, :]
            sin = jnp.sin(ang)[:, :, None, :, :]
            xr = x.reshape(b, n, h, p, half, 2)
            x1, x2 = (xr[..., 0], xr[..., 1])
            out = jnp.stack([x1 * cos - x2 * sin, x1 * sin + x2 * cos], axis=-1)
            return out.reshape(b, n, h, d)
        b, n, _ = x.shape
        ctx_n = ctx.shape[1]
        q = (x @ Wq).reshape(b, n, N_HEADS, HEAD_DIM)
        k, v = jnp.split(ctx @ Wkv, 2, axis=-1)
        k = k.reshape(b, ctx_n, N_HEADS, HEAD_DIM)
        v = v.reshape(b, ctx_n, N_HEADS, HEAD_DIM)
        q = apply_axial_rope(q, pos_map)
        k = apply_axial_rope(k, ctx_pos_map)
        scale = 1.0 / np.sqrt(HEAD_DIM).astype(np.float32)
        logits = jnp.einsum('bqhd,bkhd->bhqk', q, k) * scale
        w = jax.nn.softmax(logits, axis=-1)
        attn = jnp.einsum('bhqk,bkhd->bqhd', w, v)
        attn = attn.reshape(b, n, N_HEADS * HEAD_DIM)
        return attn @ Wout + bout

    def _L0_ffn_ref(hidden_states, gate_weight, gate_up_proj, down_proj):
        import jax, jax.numpy as jnp
        import numpy as np
        K_SKIP = 4
        NORM_TOPK = True
        B, S, H = hidden_states.shape
        E = gate_weight.shape[0]
        x = hidden_states.reshape(-1, H)
        T = x.shape[0]
        router_logits = x @ gate_weight.T
        router_probs = jax.nn.softmax(router_logits.astype(jnp.float32), axis=-1)
        router_probs = router_probs.astype(router_logits.dtype)
        top_v, top_i = jax.lax.top_k(router_probs, K_SKIP)
        if NORM_TOPK:
            top_v = top_v / jnp.clip(top_v.sum(axis=-1, keepdims=True), 1e-12)
        combine = jnp.zeros((T, E), dtype=top_v.dtype).at[jnp.arange(T)[:, None], top_i].add(top_v)

        def body(acc, expert):
            w1, w2, we = expert
            gate, up = jnp.split(x @ w1.T, 2, axis=-1)
            h = jax.nn.silu(gate) * up @ w2.T
            return (acc + h * we[:, None], None)
        out, _ = jax.lax.scan(body, jnp.zeros_like(x), (gate_up_proj, down_proj, combine.T))
        return out.reshape(B, S, H)
    x = x + _L0_xattn_ref(_layernorm(x, axis=-1), ctx_1024, fside_BxSx2_0, fside_BxSx2_0, L0_xattn_Wq, L0_xattn_Wkv, L0_xattn_Wout, L0_xattn_bout)
    x = x + _L0_ffn_ref(_layernorm(x, axis=-1), L0_ffn_gate_weight, L0_ffn_gate_up_proj, L0_ffn_down_proj)
    return x

_drawn_inputs = setup_inputs


def setup_inputs(seed=0):
    import zlib

    import numpy as np

    out = dict(_drawn_inputs(seed))
    spreads = {'L0_xattn_bout': (0.0, 0.1)}
    factors = {'L0_ffn_gate_weight': 8.0, 'L0_ffn_gate_up_proj': 8.0, 'L0_ffn_down_proj': 8.0}
    for name, (base, spread) in spreads.items():
        noise = np.random.default_rng([zlib.crc32(name.encode()), seed]).standard_normal(out[name].shape)
        drawn = base * np.exp(spread * noise) if base else spread * noise
        out[name] = jnp.asarray(drawn.astype(out[name].dtype))
    for name, factor in factors.items():
        out[name] = (out[name] * factor).astype(out[name].dtype)
    return out
```

```python
import math

import numpy as np

import concourse.bass as bass
from concourse import mybir
from contextlib import ExitStack

F32 = mybir.dt.float32
BF16 = mybir.dt.bfloat16
I32 = mybir.dt.int32
U32 = mybir.dt.uint32
ALU = mybir.AluOpType
ACT = mybir.ActivationFunctionType
AX = mybir.AxisListType

P = 128
BATCH, SEQ, DIM, CTX = 32, 64, 256, 128
HEADS, HD = 32, 8
EXPERTS, INNER, TOPK = 64, 96, 4
TOKENS = BATCH * SEQ
TILES = TOKENS // P
GROUPS = 4
HG = HEADS // GROUPS
PAIRS = HEADS // 2
PPG = PAIRS // GROUPS
EPS = 1e-5
SCALE = 1.0 / math.sqrt(HD)
TWO_PI = 2.0 * math.pi

ROW = DIM + 4
COL_DEST, COL_W, COL_EXP = DIM, DIM + 1, DIM + 2
BLOCKS = TOKENS * TOPK // P + EXPERTS
KSLOTS = TOPK + 1
BG = 4
BGROUPS = BLOCKS // BG

C_ID, C_HM, C_IOTA, C_DEST, C_TRI, C_END = 0, 128, 136, 200, 204, 332


class Chain:

    def __init__(self, eng, sem, base=0):
        self.eng, self.sem, self.base, self.n = eng, sem, base, 0

    def after(self, instruction):
        self.n += 1
        instruction.then_inc(self.sem, 1)

    def sync(self):
        self.eng.wait_ge(self.sem, self.base + self.n)


def reached(eng, sem, value):
    if not isinstance(value, int) or value > 0:
        eng.wait_ge(sem, value)


def build(nc, x_d, ctxT_d, pos_d, wq_d, wk_d, wv_d, wo_d, bout_d, gate_d, gu_d, w2_d, const_d, blank_d, out_d):
    rows_d = nc.dram_tensor("rows_d", [BLOCKS * P, ROW], F32, kind="Internal").ap()
    res_d = nc.dram_tensor("res_d", [TOKENS * KSLOTS, DIM], F32, kind="Internal").ap()
    res_tok = res_d.rearrange("(t k) d -> t k d", k=KSLOTS)

    ctx = ExitStack()
    with ctx:
        def sb(name, shape, dt=F32):
            return ctx.enter_context(nc.sbuf_tensor(name, shape, dt))

        def sem(name):
            return ctx.enter_context(nc.semaphore(name))

        gu_sb = sb("gu_sb", [P, EXPERTS, 2, 2 * INNER])
        wq_sb = sb("wq_sb", [P, 2, DIM])
        wk_sb = sb("wk_sb", [P, DIM])
        wv_sb = sb("wv_sb", [P, 2, DIM // 2])
        wo_sb = sb("wo_sb", [P, 2, DIM])
        gate_sb = sb("gate_sb", [P, 2, EXPERTS])
        bout_sb = sb("bout_sb", [P, DIM])
        const = sb("const", [P, C_END])
        blank = sb("blank", [P, ROW])
        ident = const[:, C_ID:C_ID + P]
        hmask = const[:, C_HM:C_HM + HG]
        iota_e = const[:, C_IOTA:C_IOTA + EXPERTS]
        tri = sb("tri", [P, P], BF16)
        ones_bf = sb("ones_bf", [P, P], BF16)
        ones_e = sb("ones_e", [P, EXPERTS])
        neg_half = sb("neg_half", [P, 1])

        pos_sb = sb("pos_sb", [P, TILES, 2])
        ang = sb("ang", [P, 2, TILES, 4])
        turns = sb("turns", [P, 2, TILES, 4])
        trig = sb("trig", [P, 2, TILES, 4])
        nsin = sb("nsin", [P, TILES, 4])

        xa = sb("xa", [P, 2, DIM])
        ctxT = sb("ctxT", [P, 2, P])
        st1 = sb("st1", [P, 6])
        mv1 = sb("mv1", [P, 2])
        ve1 = sb("ve1", [P, 1])
        rstd1 = sb("rstd1", [P, 1])
        xhat = sb("xhat", [P, DIM])
        xhT = sb("xhT", [P, 2, P])
        k_cos = sb("k_cos", [P, DIM])
        k_sin = sb("k_sin", [P, DIM])
        k_rot = sb("k_rot", [P, DIM])
        q_cos = sb("q_cos", [P, DIM])
        q_sin = sb("q_sin", [P, DIM])
        q_rot = sb("q_rot", [P, DIM])
        q_diag = sb("q_diag", [P, 2, GROUPS, P])
        k_mask = sb("k_mask", [P, 2, GROUPS, HG, SEQ])
        v_pair = sb("v_pair", [P, 2, 2, PAIRS, 2, HD + 1])

        mx = sb("mx", [P, 2, HG])
        shifted = sb("shifted", [P, 2, HG * SEQ])
        probT = sb("probT", [P, 2, PPG, P])

        rsum = sb("rsum", [P, HEADS])
        attn = sb("attn", [P, DIM])
        attnT = sb("attnT", [P, 2, P])
        xres = sb("xres", [P, 2, DIM])
        x2 = sb("x2", [P, 2, DIM])
        st2 = sb("st2", [P, 6])
        mv2 = sb("mv2", [P, 2])
        ve2 = sb("ve2", [P, 1])
        rstd2 = sb("rstd2", [P, 1])
        xh2 = sb("xh2", [P, DIM])
        xh2T = sb("xh2T", [P, 2, P])
        nmx = sb("nmx", [P, 1])
        expl = sb("expl", [P, EXPERTS])
        esum = sb("esum", [P, 1])
        resum = sb("resum", [P, 1])
        probs = sb("probs", [P, EXPERTS])
        top8 = sb("top8", [P, 8])
        idx8 = sb("idx8", [P, 8], U32)
        idxf = sb("idxf", [P, TOPK])
        wsum = sb("wsum", [P, 1])
        rwsum = sb("rwsum", [P, 1])
        chosen = sb("chosen", [P, 2, TOPK, EXPERTS])
        taken = sb("taken", [P, 2, EXPERTS], BF16)
        rows = sb("rows", [P, 2, TOPK, ROW])

        count = sb("count", [P, EXPERTS])
        room = sb("room", [P, EXPERTS])
        base = sb("base", [P, EXPERTS])
        nblocks = sb("nblocks", [P, 1])
        rank = sb("rank", [P, EXPERTS])
        opens = sb("opens", [P, EXPERTS])
        upto = sb("upto", [P, EXPERTS])
        newest = sb("newest", [P, EXPERTS])
        fresh = sb("fresh", [P, EXPERTS])
        step_b = sb("step_b", [P, EXPERTS])
        spill = sb("spill", [P, EXPERTS])
        slot_e = sb("slot_e", [P, EXPERTS])
        slot_ke = sb("slot_ke", [P, TOPK, EXPERTS])
        slot_k = sb("slot_k", [P, TOPK])
        slot_i = sb("slot_i", [P, 2, TOPK], I32)
        dest = sb("dest", [P, TOPK])

        xb = sb("xb", [P, 2, BG, ROW])
        w2_sb = sb("w2_sb", [INNER, BG, DIM])
        xbT = sb("xbT", [P, 2, 2, P])
        silu = sb("silu", [P, 2, INNER])
        hid = sb("hid", [P, 2, INNER])
        hidT = sb("hidT", [INNER, 2, P])
        yb = sb("yb", [P, BG, DIM])

        NRES = 4
        gu_flat = gu_sb[:].rearrange("p e c n -> p (e c n)")
        res_cols = NRES * KSLOTS * DIM
        res = gu_flat[:, 0:res_cols].rearrange("p (j k d) -> p j k d", j=NRES, k=KSLOTS)
        fin = gu_flat[:, res_cols:res_cols + NRES * DIM].rearrange("p (j d) -> p j d", j=NRES)

        bank = [ctx.enter_context(nc.psum_tensor(f"bank{i}", [P, 512], F32)) for i in range(8)]
        ps_q, ps_kv, ps_o, ps_c = bank[0], bank[1], bank[6], bank[7]
        ps_s, ps_t = bank[2:4], bank[4:6]
        o_view = ps_o[:, 0:PAIRS * 2 * (HD + 1)].rearrange("p (h d) -> p h d", d=HD + 1)
        RANK = 320
        pp_xT, pp_gu, pp_hT, pp_y = bank[0:2], bank[2:4], bank[4:6], bank[6:8]

        consts_in = sem("consts_in"); pos_in = sem("pos_in")
        consts_ready = sem("consts_ready"); dve_const = sem("dve_const")
        angles_ready = sem("angles_ready"); trig_ready = sem("trig_ready"); nsin_ready = sem("nsin_ready")
        blank_rows = sem("blank_rows")
        gu_in = sem("gu_in")
        xa_in = [sem(f"xa_in{p}") for p in range(2)]
        xres_in = [sem(f"xres_in{p}") for p in range(2)]
        var1_ready = sem("var1_ready"); rstd1_ready = sem("rstd1_ready"); xhat_ready = sem("xhat_ready")
        xT_done = sem("xT_done"); xhT_ready = sem("xhT_ready")
        kv_done = sem("kv_done"); q_done = sem("q_done")
        kparts_ready = sem("kparts_ready"); qparts_ready = sem("qparts_ready")
        k_ready = sem("k_ready"); q_ready = sem("q_ready")
        qkT_done = sem("qkT_done")
        qdiag_ready = sem("qdiag_ready"); kmask_ready = sem("kmask_ready"); v_ready = sem("v_ready")
        s_done = sem("s_done"); max_ready = sem("max_ready"); shifted_ready = sem("shifted_ready")
        t_done = sem("t_done"); prob_ready = sem("prob_ready"); av_done = sem("av_done")
        rsum_ready = sem("rsum_ready"); attn_ready = sem("attn_ready")
        aT_done = sem("aT_done"); attnT_ready = sem("attnT_ready"); wo_done = sem("wo_done")
        xres_ready = sem("xres_ready"); x2_ready = sem("x2_ready")
        x2_stored = [sem(f"x2_stored{p}") for p in range(2)]
        var2_ready = sem("var2_ready"); rstd2_ready = sem("rstd2_ready"); xh2_ready = sem("xh2_ready")
        x2T_done = sem("x2T_done"); xh2T_ready = sem("xh2T_ready"); router_done = sem("router_done")
        nmx_ready = sem("nmx_ready"); expl_ready = sem("expl_ready")
        taken_ready = sem("taken_ready"); rank_done = sem("rank_done"); rank_read = sem("rank_read"); slot_ready = sem("slot_ready")
        rowvals_ready = sem("rowvals_ready")
        scattered = [sem(f"scattered{p}") for p in range(2)]
        dve_step = sem("dve_step")
        passed = sem("passed")
        xb_in = [sem(f"xb_in{p}") for p in range(2)]
        w2_in = [sem(f"w2_in{j}") for j in range(BG)]
        xbT_done = sem("xbT_done"); xbT_ready = sem("xbT_ready"); gu_done = sem("gu_done")
        silu_ready = sem("silu_ready"); hid_ready = sem("hid_ready"); hT_done = sem("hT_done")
        hidT_ready = sem("hidT_ready"); y_done = sem("y_done"); yb_ready = sem("yb_ready")
        y_scattered = [sem(f"y_scattered{j}") for j in range(BG)]
        res_in = [sem(f"res_in{j}") for j in range(NRES)]
        fin_ready = sem("fin_ready")
        fin_out = [sem(f"fin_out{j}") for j in range(NRES)]

        def alone(eng):
            eng.sem_inc(passed, 1)

        INIT = BLOCKS // 8
        GU_STEP = EXPERTS // (TILES - 6)
        GU_REST = EXPERTS - GU_STEP * (TILES - 6)

        def pipeline(eng, step):
            def stages(i):
                on = set()
                if i + 1 < TILES:
                    on.add("L")
                for name, lag in (("A", 0), ("B", 1), ("C", 2), ("D", 3)):
                    if 0 <= i - lag < TILES:
                        on.add(name)
                return on

            for i in range(4):
                step(i, i % 2, i // 2, stages(i))
            with eng.Fori(2, TILES // 2 - 1) as twos:
                i = twos * 2
                step(i, 0, twos, set("LABCD"))
                step(i + 1, 1, twos, set("LABCD"))
            for i in range(TILES - 2, TILES + 3):
                step(i, i % 2, i // 2, stages(i))

        def earlier(twos, p, lag):
            return twos + (p - lag) // 2

        block = ctx.enter_context(nc.Block())

        @block.sync
        def _(sp):
            sp.dma_start(pos_sb[:], pos_d.rearrange("(t p) a -> p t a", p=P)).then_inc(pos_in, 16)
            sp.dma_start(const[:], const_d).then_inc(consts_in, 16)
            sp.dma_start(blank[:], blank_d).then_inc(consts_in, 16)
            sp.dma_start(wk_sb[:], wk_d).then_inc(consts_in, 16)
            sp.dma_start(wv_sb[:], wv_d).then_inc(consts_in, 16)
            sp.dma_start(wq_sb[:], wq_d).then_inc(consts_in, 16)
            sp.dma_start(wo_sb[:], wo_d).then_inc(consts_in, 16)
            sp.dma_start(gate_sb[:], gate_d).then_inc(consts_in, 16)
            sp.dma_start(bout_sb[:], bout_d).then_inc(consts_in, 16)

            def load_tile(i, p):
                reached(sp, xhat_ready, i - 1)
                reached(sp, kv_done, i - 1)
                sp.dma_start(xa[:, p, :], x_d[bass.ds(i * P, P), :]).then_inc(xa_in[p], 16)
                sp.dma_start(ctxT[:, p, :], ctxT_d[:, bass.ds(i * P, P)]).then_inc(xa_in[p], 16)

            def load_residual(i, p):
                reached(sp, x2_ready, i - 1)
                sp.dma_start(xres[:, p, :], x_d[bass.ds(i * P, P), :]).then_inc(xres_in[p], 16)

            load_tile(0, 0)
            load_tile(1, 1)
            load_residual(0, 0)
            load_residual(1, 1)
            sp.wait_ge(consts_in, 16 * 8)
            view = rows_d.rearrange("(b p) c -> p b c", p=P)

            def blank_part(k):
                sp.dma_start(view[:, k * INIT:(k + 1) * INIT, :],
                             blank[:].unsqueeze(1).to_broadcast([P, INIT, ROW])).then_inc(blank_rows, 16)

            blank_part(0)
            blank_part(1)

            def store_x2(i, p):
                sp.wait_ge(x2_ready, i + 1)
                sp.dma_start(res_tok[bass.ds(i * P, P), TOPK, :], x2[:, p, :]).then_inc(x2_stored[p], 16)

            def step(i, p, twos, on):
                if isinstance(i, int) is False or i + 2 < TILES:
                    load_tile(i + 2, p)
                if "C" in on:
                    store_x2(i - 2, p)
                    if isinstance(i, int) is False or i < TILES:
                        load_residual(i, p)

            def load_gate_up(e, n):
                sp.dma_start(gu_sb[:, bass.ds(e, n)], gu_d[:, bass.ds(e, n)]).then_inc(gu_in, 16)

            for i in range(4):
                step(i, i % 2, i // 2, {"C"} if i >= 2 else set())
                if i < 3:
                    blank_part(2 * i + 2)
                    blank_part(2 * i + 3)
                else:
                    load_gate_up(EXPERTS - GU_REST, GU_REST)
            with sp.Fori(2, TILES // 2 - 1) as twos:
                i = twos * 2
                step(i, 0, twos, {"C"})
                load_gate_up((i - 4) * GU_STEP, GU_STEP)
                step(i + 1, 1, twos, {"C"})
                load_gate_up((i - 3) * GU_STEP, GU_STEP)
            for i in range(TILES - 2, TILES + 2):
                step(i, i % 2, i // 2, {"C"})

            for p in range(2):
                sp.wait_ge(scattered[p], 16 * TOPK * TILES // 2)

            grp = rows_d.rearrange("(g j p) c -> g p j c", p=P, j=BG)

            def load_group(g, p):
                reached(sp, yb_ready, (g - 1) * BG)
                alone(sp)
                if isinstance(g, int) is False or g >= 2:
                    for j in range(BG):
                        sp.wait_ge(y_scattered[j], (g - 1) * 16)
                sp.dma_start(xb[:, p, :, :], grp[bass.ds(g, 1)].rearrange("g p j c -> (g p) j c")).then_inc(xb_in[p], 16)

            def load_down(g, p, h):
                sp.wait_ge(xb_in[p], (h + 1) * 16)
                alone(sp)
                for j in range(BG):
                    e = sp.value_load(xb[0:1, p, j, COL_EXP:COL_EXP + 1].bitcast(I32), min_val=0, max_val=EXPERTS - 1)
                    reached(sp, y_done, (g - 1) * BG + j + 1)
                    sp.dma_start(w2_sb[:, j, :], w2_d[bass.ds(e, 1)].rearrange("e i d -> (e i) d")).then_inc(w2_in[j], 16)

            load_group(0, 0)
            load_group(1, 1)
            load_down(0, 0, 0)
            load_down(1, 1, 0)
            with sp.Fori(1, BGROUPS // 2) as twos:
                g = twos * 2
                load_group(g, 0)
                load_down(g, 0, twos)
                load_group(g + 1, 1)
                load_down(g + 1, 1, twos)

            for j in range(BG):
                sp.wait_ge(y_scattered[j], BGROUPS * 16)
            for p in range(2):
                sp.wait_ge(x2_stored[p], 16 * TILES // 2)

            def load_results(i, j):
                reached(sp, fin_ready, i - NRES + 1)
                sp.dma_start(res[:, j], res_tok[bass.ds(i * P, P)]).then_inc(res_in[j], 16)

            for j in range(NRES):
                load_results(j, j)
            with sp.Fori(1, TILES // NRES) as fours:
                i = fours * NRES
                for j in range(NRES):
                    load_results(i + j, j)

        @block.gpsimd
        def _(pool):
            g = nc.gpsimd
            g.memset(neg_half[:], -0.5).then_inc(consts_ready, 1)
            g.memset(ones_e[:], 1.0).then_inc(consts_ready, 1)
            g.memset(ones_bf[:], 1.0).then_inc(consts_ready, 1)
            g.memset(q_diag[:], 0.0).then_inc(consts_ready, 1)
            g.memset(v_pair[:], 0.0).then_inc(consts_ready, 1)
            pool.wait_ge(consts_ready, 5)
            for h in range(2):
                r = slice(h * SEQ, (h + 1) * SEQ)
                g.memset(v_pair[r, :, :, :, h, HD:HD + 1].rearrange("p s b n o -> p (s b n) o"), 1.0).then_inc(consts_ready, 1)

            def rstd(var, out, ready, n, done):
                pool.wait_ge(ready, n)
                g.tensor_tensor(out[:], var[:], neg_half[:], ALU.pow).then_inc(done, 1)

            def step(i, p, twos, on):
                if "D" in on:
                    d = 1 - p
                    pool.wait_ge(rowvals_ready, i - 2)
                if "A" in on:
                    pool.wait_ge(kparts_ready, i + 1)
                    reached(pool, qkT_done, i)
                    g.tensor_tensor(k_rot[:], k_cos[:], k_sin[:], ALU.add).then_inc(k_ready, 1)
                    pool.wait_ge(qparts_ready, i + 1)
                    g.tensor_tensor(q_rot[:], q_cos[:], q_sin[:], ALU.add).then_inc(q_ready, 1)
                if "D" in on:
                    pool.wait_ge(slot_ready, i - 2)
                    if isinstance(i, int) and i == 3:
                        pool.wait_ge(blank_rows, 16 * -(-EXPERTS // INIT))
                    for k in range(2):
                        scatter(d, k)
                if "C" in on:
                    rstd(ve2, rstd2, var2_ready, i - 1, rstd2_ready)
                if "D" in on:
                    for k in range(2, TOPK):
                        scatter(d, k)
                    if isinstance(i, int) and i == 3:
                        pool.wait_ge(blank_rows, 16 * 8)
                if "L" in on:
                    rstd(ve1, rstd1, var1_ready, i + 2, rstd1_ready)
                if "B" in on:
                    pool.wait_ge(xres_in[1 - p], 16 * (earlier(twos, p, 1) + 1))
                    g.tensor_tensor(xres[:, 1 - p, :], xres[:, 1 - p, :], bout_sb[:], ALU.add).then_inc(xres_ready, 1)

            def scatter(d, k):
                alone(pool)
                g.indirect_dma_start(rows_d, bass.IndirectOffsetOnAxis(ap=slot_i[:, d, k:k + 1], axis=0),
                                     rows[:, d, k, :], None).then_inc(scattered[d], 16)

            pool.wait_ge(consts_in, 16 * 8)
            rstd(ve1, rstd1, var1_ready, 1, rstd1_ready)
            pipeline(pool, step)

            def scatter_block(b, p, j):
                pool.wait_ge(yb_ready, b + 1)
                alone(pool)
                g.indirect_dma_start(res_d, bass.IndirectOffsetOnAxis(ap=xb[:, p, j, COL_DEST:COL_DEST + 1].bitcast(I32), axis=0),
                                     yb[:, j, :], None, bounds_check=TOKENS * KSLOTS - 1, oob_is_err=False).then_inc(y_scattered[j], 16)

            with pool.Fori(0, BLOCKS // (2 * BG)) as eights:
                b = eights * (2 * BG)
                for p in range(2):
                    for j in range(BG):
                        scatter_block(b + p * BG + j, p, j)

        @block.scalar
        def _(act):
            a = nc.scalar
            act.wait_ge(angles_ready, 1)
            a.activation(trig[:], ang[:], ACT.Sin).then_inc(trig_ready, 1)

            def kmask_part(i, p, hs):
                for h in hs:
                    m = a.activation(k_mask[:, p, :, h, :], ps_q[:, 256:512].rearrange("p (g k) -> p g k", g=GROUPS),
                                     ACT.Copy, scale=hmask[:, h:h + 1])
                return m

            def exp_group(i, g):
                n = i * GROUPS + g
                act.wait_ge(t_done, n + 1)
                reached(act, av_done, n - 1)
                a.activation(probT[:, g % 2].rearrange("p j q -> p (j q)"), ps_t[g % 2][:], ACT.Exp,
                             scale=SCALE).then_inc(prob_ready, 1)

            def step(i, p, twos, on):
                if "A" in on:
                    act.wait_ge(xT_done, i + 1)
                    reached(act, q_done, i)
                    a.copy(xhT[:].rearrange("p c t -> p (c t)"), ps_q[:, 0:256]).then_inc(xhT_ready, 1)
                if "C" in on:
                    act.wait_ge(aT_done, i - 1)
                    reached(act, wo_done, i - 2)
                    a.copy(attnT[:].rearrange("p c t -> p (c t)"), ps_c[:, 0:256]).then_inc(attnT_ready, 1)
                if "A" in on:
                    act.wait_ge(kparts_ready, i + 1)
                    if not isinstance(i, int) or i >= 2:
                        act.wait_ge(av_done, GROUPS * (i - 1))
                    for h in range(2):
                        r = slice(h * SEQ, (h + 1) * SEQ)
                        m = a.copy(v_pair[r, p, :, :, h, 0:HD],
                                   ps_kv[r, 256:512].rearrange("p (b n d) -> p b n d", b=2, d=HD))
                    m.then_inc(v_ready, 1)
                if "B" in on:
                    exp_group(i - 1, 0)
                    exp_group(i - 1, 1)
                    exp_group(i - 1, 2)
                if "A" in on:
                    act.wait_ge(qkT_done, i + 1)
                    if not isinstance(i, int) or i >= 2:
                        act.wait_ge(s_done, GROUPS * (i - 1))
                    for b in range(2):
                        r = slice(b * SEQ, (b + 1) * SEQ)
                        m = a.copy(q_diag[r, p, :, r], ps_q[r, 0:256].rearrange("p (g q) -> p g q", g=GROUPS))
                    m.then_inc(qdiag_ready, 1)
                    kmask_part(i, p, range(0, 3))
                if "C" in on:
                    act.wait_ge(x2T_done, i - 1)
                    reached(act, router_done, i - 2)
                    a.copy(xh2T[:].rearrange("p c t -> p (c t)"), ps_c[:, 0:256]).then_inc(xh2T_ready, 1)
                if "B" in on:
                    exp_group(i - 1, 3)
                if "A" in on:
                    kmask_part(i, p, range(3, HG)).then_inc(kmask_ready, 1)
                if "C" in on:
                    if not isinstance(i, int) or i >= 4:
                        act.wait_ge(scattered[p], 16 * TOPK * earlier(twos, p, 2))
                    act.wait_ge(nmx_ready, i - 1)
                    a.activation(expl[:], ps_c[:, 256:256 + EXPERTS], ACT.Exp, bias=nmx[:, 0:1],
                                 accum_out=esum[:, 0:1]).then_inc(expl_ready, 1)
                    for k in range(TOPK):
                        m = a.copy(rows[:, p, k, 0:DIM], xh2[:])
                    m.then_inc(rowvals_ready, 1)

            act.wait_ge(consts_in, 16 * 8)
            act.wait_ge(consts_ready, 7)
            pipeline(act, step)

            def silu_block(b, u, rnd):
                p = u % 2
                act.wait_ge(gu_done, b + 1)
                reached(act, hid_ready, b - 1)
                a.activation(silu[:, p, :], pp_gu[p][:, 0:INNER], ACT.Silu).then_inc(silu_ready, 1)

            def hidT_block(b, u, rnd):
                p = u % 2
                act.wait_ge(hT_done, b + 1)
                reached(act, y_done, b - 1)
                a.copy(hidT[:, p, :], pp_hT[p][0:INNER, 0:P]).then_inc(hidT_ready, 1)

            def weigh_block(b, u, rnd):
                gp, j, p = u // BG % 2, u % BG, u % 2
                act.wait_ge(y_done, b + 1)
                if not isinstance(b, int) or b >= BG:
                    act.wait_ge(y_scattered[j], (rnd * 2 + u // BG) * 16)
                a.activation(yb[:, j, :], pp_y[p][:, 0:DIM], ACT.Copy,
                             scale=xb[:, gp, j, COL_W:COL_W + 1]).then_inc(yb_ready, 1)

            beats2(act, {1: silu_block, 2: hidT_block,
                         3: weigh_block})

            def store(i, j):
                act.wait_ge(fin_ready, i + 1)
                act.dma_start(out_d[bass.ds(i * P, P), :], fin[:, j, :]).then_inc(fin_out[j], 16)

            for j in range(NRES):
                store(j, j)
            with act.Fori(1, TILES // NRES) as fours:
                i = fours * NRES
                for j in range(NRES):
                    store(i + j, j)
            for j in range(NRES):
                act.wait_ge(fin_out[j], 16 * TILES // NRES)

        @block.vector
        def _(dve):
            v = nc.vector
            prep = Chain(dve, dve_const)

            def link(instruction):
                prep.after(instruction)
                prep.sync()

            dve.wait_ge(pos_in, 16)
            for axis in range(2):
                for f in range(2):
                    m = v.tensor_scalar(ang[:, 0, :, 2 * axis + f], pos_sb[:, :, axis], 10000.0 ** (-f / 2), None, ALU.mult)
            link(m)
            link(v.tensor_scalar(ang[:, 1], ang[:, 0], math.pi / 2, None, ALU.add))
            ROUND = 1.5 * 2.0 ** 23
            HI = 6.28125
            link(v.tensor_scalar(turns[:], ang[:], 1.0 / TWO_PI, ROUND, ALU.mult, ALU.add))
            link(v.tensor_scalar(turns[:], turns[:], ROUND, None, ALU.subtract))
            link(v.scalar_tensor_tensor(ang[:], turns[:], -HI, ang[:], ALU.mult, ALU.add))
            link(v.scalar_tensor_tensor(ang[:], turns[:], -(TWO_PI - HI), ang[:], ALU.mult, ALU.add))
            v.tensor_scalar(ang[:], ang[:], 3.1415925, -3.1415925, ALU.min, ALU.max).then_inc(angles_ready, 1)
            dve.wait_ge(consts_in, 16 * 8)
            v.tensor_copy(tri[:], const[:, C_TRI:C_TRI + P])
            v.tensor_copy(dest[:], const[:, C_DEST:C_DEST + TOPK])
            v.memset(count[:], 0.0)
            v.memset(room[:], 0.0)
            v.memset(base[:], 0.0)
            v.memset(nblocks[:], 0.0)
            v.memset(rows[:], 0.0)
            dve.wait_ge(trig_ready, 1)
            link(v.tensor_scalar(nsin[:], trig[:, 0], -1.0, None, ALU.mult))
            dve.wait_ge(consts_ready, 7)

            def bc(table, i):
                return table[:, bass.ds(i, 1), :]

            def rotate(src, cos_out, sin_out, i):
                s = src.rearrange("p (h c two) -> p h c two", c=4, two=2)
                oc = cos_out[:].rearrange("p (h c two) -> p h c two", c=4, two=2)
                os_ = sin_out[:].rearrange("p (h c two) -> p h c two", c=4, two=2)
                cos = trig[:, 1, bass.ds(i, 1), :].unsqueeze(3).to_broadcast([P, HEADS, 4, 2])
                v.tensor_tensor(oc, s, cos, ALU.mult)
                sin_e = nsin[:, bass.ds(i, 1), :].to_broadcast([P, HEADS, 4])
                sin_o = trig[:, 0, bass.ds(i, 1), :].to_broadcast([P, HEADS, 4])
                v.tensor_tensor(os_[:, :, :, 0], s[:, :, :, 1], sin_e, ALU.mult)
                return v.tensor_tensor(os_[:, :, :, 1], s[:, :, :, 0], sin_o, ALU.mult)

            def shift_group(i, g, ch):
                n = i * GROUPS + g
                s = ps_s[g % 2][:].rearrange("p (h k) -> p h k", h=HG)
                dve.wait_ge(s_done, n + 1)
                v.tensor_reduce(mx[:, g % 2, :], s, AX.X, ALU.max).then_inc(max_ready, 1)
                dve.wait_ge(max_ready, n + 1)
                reached(dve, t_done, n - 1)
                v.tensor_tensor(shifted[:, g % 2, :].rearrange("p (h k) -> p h k", h=HG), s,
                                mx[:, g % 2, :].unsqueeze(2).to_broadcast([P, HG, SEQ]),
                                ALU.subtract).then_inc(shifted_ready, 1)

            def stats(ch, src, st, mv, ve, ready):
                ch.after(v.bn_stats(st[:], src))
                ch.sync()
                alone(dve)
                ch.after(v.bn_aggr(mv[:], st[:]))
                ch.sync()
                v.tensor_scalar(ve[:], mv[:, 1:2], EPS, None, ALU.add).then_inc(ready, 1)

            def norm(dst, src, mv, rstd):
                return v.tensor_scalar(dst, src, mv[:, 0:1], rstd[:, 0:1], ALU.subtract, ALU.mult)

            def ln1_stats(i, p, before, ch):
                dve.wait_ge(xa_in[p], 32 * (before + 1))
                stats(ch, xa[:, p, :], st1, mv1, ve1, var1_ready)

            def ln1_apply(i, p):
                dve.wait_ge(rstd1_ready, i + 1)
                reached(dve, xT_done, i)
                norm(xhat[:], xa[:, p, :], mv1, rstd1).then_inc(xhat_ready, 1)

            def step(i, p, twos, on, base_n):
                ch = Chain(dve, dve_step, base_n)
                if "C" in on:
                    c = i - 2
                    dve.wait_ge(av_done, GROUPS * (i - 1))
                    v.reciprocal(rsum[:], o_view[:, :, HD]).then_inc(rsum_ready, 1)
                    dve.wait_ge(rsum_ready, i - 1)
                    reached(dve, aT_done, i - 2)
                    v.tensor_tensor(attn[:].rearrange("p (h d) -> p h d", d=HD), o_view[:, :, 0:HD],
                                    rsum[:].unsqueeze(2).to_broadcast([P, HEADS, HD]), ALU.mult).then_inc(attn_ready, 1)
                if "B" in on:
                    shift_group(i - 1, 0, ch)
                    shift_group(i - 1, 1, ch)
                if "A" in on:
                    dve.wait_ge(kv_done, i + 1)
                    reached(dve, k_ready, i)
                    rotate(ps_kv[:, 0:256], k_cos, k_sin, i).then_inc(kparts_ready, 1)
                    dve.wait_ge(q_done, i + 1)
                    reached(dve, q_ready, i)
                    rotate(ps_q[:, 256:512], q_cos, q_sin, i).then_inc(qparts_ready, 1)
                if "D" in on:
                    slots(i, 1 - p, earlier(twos, p, 3), ch)
                if "B" in on:
                    shift_group(i - 1, 2, ch)
                if "C" in on:
                    dve.wait_ge(wo_done, i - 1)
                    dve.wait_ge(xres_ready, i - 1)
                    if not isinstance(i, int) or i >= 4:
                        dve.wait_ge(x2_stored[p], 16 * earlier(twos, p, 2))
                    v.tensor_tensor(x2[:, p, :], ps_c[:, 256:512], xres[:, p, :], ALU.add).then_inc(x2_ready, 1)
                    dve.wait_ge(x2_ready, i - 1)
                    stats(ch, x2[:, p, :], st2, mv2, ve2, var2_ready)
                if "B" in on:
                    shift_group(i - 1, 3, ch)
                if "C" in on:
                    dve.wait_ge(rstd2_ready, i - 1)
                    reached(dve, rowvals_ready, i - 2)
                    reached(dve, x2T_done, i - 2)
                    norm(xh2[:], x2[:, p, :], mv2, rstd2).then_inc(xh2_ready, 1)
                if "L" in on:
                    ln1_stats(i + 1, 1 - p, earlier(twos, p, -1), ch)
                if "L" in on:
                    ln1_apply(i + 1, 1 - p)
                if "C" in on:
                    route(i, p, ch)
                return ch.n

            def route(i, p, ch):
                def link(x):
                    ch.after(x)
                    ch.sync()

                dve.wait_ge(router_done, i - 1)
                v.tensor_reduce(nmx[:], ps_c[:, 256:256 + EXPERTS], AX.X, ALU.max, negate=True).then_inc(nmx_ready, 1)
                dve.wait_ge(expl_ready, i - 1)
                link(v.reciprocal(resum[:], esum[:]))
                link(v.tensor_scalar(probs[:], expl[:], resum[:, 0:1], None, ALU.mult))
                alone(dve)
                link(v.max(top8[:], probs[:]))
                alone(dve)
                ch.after(v.max_index(idx8[:], top8[:], probs[:]))
                link(v.tensor_reduce(wsum[:], top8[:, 0:TOPK], AX.X, ALU.add))
                ch.after(v.tensor_copy(idxf[:], idx8[:, 0:TOPK]))
                link(v.tensor_scalar(wsum[:], wsum[:], 1e-12, None, ALU.max))
                link(v.reciprocal(rwsum[:], wsum[:]))
                dve.wait_ge(rowvals_ready, i - 1)
                v.tensor_scalar(rows[:, p, :, COL_W], top8[:, 0:TOPK], rwsum[:, 0:1], None, ALU.mult)
                v.tensor_copy(rows[:, p, :, COL_EXP].bitcast(I32), idx8[:, 0:TOPK])
                v.tensor_copy(rows[:, p, :, COL_DEST].bitcast(I32), dest[:])
                link(v.tensor_tensor(chosen[:, p], iota_e.unsqueeze(1).to_broadcast([P, TOPK, EXPERTS]),
                                     idxf[:].unsqueeze(2).to_broadcast([P, TOPK, EXPERTS]), ALU.is_equal))
                link(v.tensor_scalar(dest[:], dest[:], float(P * KSLOTS), None, ALU.add))
                with nc.allow_low_precision(reason="zeros and ones"):
                    v.tensor_reduce(taken[:, p, :], chosen[:, p].rearrange("p k e -> p e k"), AX.X, ALU.add).then_inc(taken_ready, 1)

            def slots(i, p, before, ch):
                def link(x):
                    ch.after(x)
                    ch.sync()

                dve.wait_ge(rank_done, i - 2)
                v.tensor_tensor(rank[:], ps_o[:, RANK:RANK + EXPERTS], count[:], ALU.add)
                v.tensor_tensor(count[:], ps_o[:, RANK + EXPERTS:RANK + 2 * EXPERTS], count[:], ALU.add).then_inc(rank_read, 1)
                dve.wait_ge(rank_read, i - 2)
                ch.after(v.tensor_tensor(spill[:], rank[:], room[:], ALU.is_ge))
                link(v.tensor_tensor(opens[:], count[:], room[:], ALU.is_gt))
                link(v.tensor_tensor_scan(upto[:], ones_e[:], opens[:], nblocks[:, 0:1], ALU.mult, ALU.add))
                ch.after(v.tensor_copy(nblocks[:], upto[:, EXPERTS - 1:EXPERTS]))
                link(v.tensor_tensor(newest[:], upto[:], opens[:], ALU.subtract))
                link(v.scalar_tensor_tensor(fresh[:], newest[:], float(P), room[:], ALU.mult, ALU.subtract))
                ch.after(v.tensor_tensor(slot_e[:], rank[:], base[:], ALU.add))
                link(v.tensor_tensor(step_b[:], fresh[:], base[:], ALU.subtract))
                ch.after(v.tensor_tensor(spill[:], spill[:], step_b[:], ALU.mult))
                link(v.tensor_tensor(step_b[:], step_b[:], opens[:], ALU.mult))
                ch.after(v.tensor_tensor(slot_e[:], slot_e[:], spill[:], ALU.add))
                ch.after(v.tensor_tensor(base[:], base[:], step_b[:], ALU.add))
                link(v.scalar_tensor_tensor(room[:], opens[:], float(P), room[:], ALU.mult, ALU.add))
                link(v.tensor_tensor(slot_ke[:], chosen[:, p], slot_e[:].unsqueeze(1).to_broadcast([P, TOPK, EXPERTS]), ALU.mult))
                link(v.tensor_reduce(slot_k[:], slot_ke[:], AX.X, ALU.add))
                if not isinstance(i, int) or i >= 5:
                    dve.wait_ge(scattered[p], 16 * TOPK * before)
                v.tensor_copy(slot_i[:, p, :], slot_k[:]).then_inc(slot_ready, 1)

            total = 0
            n0 = Chain(dve, dve_step, 0)
            ln1_stats(0, 0, 0, n0)
            ln1_apply(0, 0)
            total = n0.n

            def stages(i):
                on = set("L") if i + 1 < TILES else set()
                return on | {s for s, lag in (("A", 0), ("B", 1), ("C", 2), ("D", 3)) if 0 <= i - lag < TILES}

            for i in range(4):
                total += step(i, i % 2, i // 2, stages(i), total)
            start = total
            FULL = CHAIN_FULL
            with dve.Fori(2, TILES // 2 - 1) as twos:
                i = twos * 2
                b0 = twos * (2 * FULL) + (start - 4 * FULL)
                n = step(i, 0, twos, set("LABCD"), b0)
                n2 = step(i + 1, 1, twos, set("LABCD"), b0 + FULL)
                assert n == FULL and n2 == FULL, (n, n2)
            total = start + FULL * (TILES - 6)
            for i in range(TILES - 2, TILES + 3):
                total += step(i, i % 2, i // 2, stages(i), total)

            def xbT_block(b, u, rnd):
                p = u % 2
                dve.wait_ge(xbT_done, b + 1)
                reached(dve, gu_done, b - 1)
                v.tensor_copy(xbT[:, p].rearrange("p c t -> p (c t)"), pp_xT[p][:, 0:DIM]).then_inc(xbT_ready, 1)

            def hid_block(b, u, rnd):
                p = u % 2
                dve.wait_ge(silu_ready, b + 1)
                reached(dve, hT_done, b - 1)
                v.tensor_tensor(hid[:, p, :], pp_gu[p][:, INNER:2 * INNER], silu[:, p, :], ALU.mult).then_inc(hid_ready, 1)

            beats2(dve, {0: xbT_block, 1: hid_block})

            def finish(i, j, k):
                dve.wait_ge(res_in[j], (k + 1) * 16)
                if not isinstance(i, int):
                    dve.wait_ge(fin_out[j], k * 16)
                v.tensor_reduce(fin[:, j, :], res[:, j].rearrange("p k d -> p d k"), AX.X, ALU.add).then_inc(fin_ready, 1)

            for j in range(NRES):
                finish(j, j, 0)
            with dve.Fori(1, TILES // NRES) as fours:
                i = fours * NRES
                for j in range(NRES):
                    finish(i + j, j, fours)

        @block.tensor
        def _(pe):
            t = nc.tensor

            def mm(out, lhsT, rhs, start=True, stop=True):
                return t.matmul(out, lhsT, rhs, start=start, stop=stop)

            def two_transposes(ps, src):
                for c in range(2):
                    m = t.transpose(ps[:, c * P:(c + 1) * P], src[:, c * P:(c + 1) * P], ident)
                return m

            def project(ps, lhsT, w):
                for c in range(2):
                    m = mm(ps, lhsT[:, c, :], w[:, c, :], start=c == 0, stop=c == 1)
                return m

            def scores(i, p, g):
                n = i * GROUPS + g
                if g == 0:
                    pe.wait_ge(qdiag_ready, i + 1)
                    pe.wait_ge(kmask_ready, i + 1)
                reached(pe, shifted_ready, n - 1)
                mm(ps_s[g % 2][:], q_diag[:, p, g, :], k_mask[:, p, g].rearrange("p h k -> p (h k)")).then_inc(s_done, 1)

            def turn(i, g):
                n = i * GROUPS + g
                pe.wait_ge(shifted_ready, n + 1)
                reached(pe, prob_ready, n - 1)
                for j in range(PPG):
                    m = t.transpose(ps_t[g % 2][:, j * P:(j + 1) * P], shifted[:, g % 2, j * P:(j + 1) * P], ident)
                m.then_inc(t_done, 1)

            def values(i, p, g):
                n = i * GROUPS + g
                pe.wait_ge(prob_ready, n + 1)
                if g == 0:
                    pe.wait_ge(v_ready, i + 1)
                    reached(pe, attn_ready, i)
                    reached(pe, rank_read, i - 1)
                for j in range(PPG):
                    pair = g * PPG + j
                    for b in range(2):
                        r = slice(b * SEQ, (b + 1) * SEQ)
                        m = mm(ps_o[r, pair * 18:(pair + 1) * 18], probT[:, g % 2, j, r],
                               v_pair[:, p, b, pair].rearrange("p h d -> p (h d)"))
                m.then_inc(av_done, 1)

            def step(i, p, twos, on):
                if "B" in on:
                    scores(i - 1, 1 - p, 0)
                if "A" in on:
                    pe.wait_ge(xhat_ready, i + 1)
                    reached(pe, kmask_ready, i)
                    two_transposes(ps_q[:, 0:256], xhat).then_inc(xT_done, 1)
                if "B" in on:
                    scores(i - 1, 1 - p, 1)
                if "C" in on:
                    pe.wait_ge(attn_ready, i - 1)
                    reached(pe, expl_ready, i - 2)
                    two_transposes(ps_c[:, 0:256], attn).then_inc(aT_done, 1)
                if "D" in on:
                    pe.wait_ge(taken_ready, i - 2)
                    mm(ps_o[:, RANK:RANK + EXPERTS], tri[:], taken[:, 1 - p, :])
                    mm(ps_o[:, RANK + EXPERTS:RANK + 2 * EXPERTS], ones_bf[:], taken[:, 1 - p, :]).then_inc(rank_done, 1)
                if "A" in on:
                    reached(pe, kparts_ready, i)
                    reached(pe, v_ready, i)
                    mm(ps_kv[:, 0:256], ctxT[:, p, :], wk_sb[:])
                    for h in range(2):
                        for b in range(2):
                            m = mm(ps_kv[h * SEQ:(h + 1) * SEQ, 256 + b * P:256 + (b + 1) * P],
                                   ctxT[:, p, b * SEQ:(b + 1) * SEQ], wv_sb[:, h, :])
                    m.then_inc(kv_done, 1)
                if "B" in on:
                    turn(i - 1, 0)
                if "A" in on:
                    pe.wait_ge(xhT_ready, i + 1)
                    project(ps_q[:, 256:512], xhT, wq_sb).then_inc(q_done, 1)
                if "B" in on:
                    scores(i - 1, 1 - p, 2)
                if "C" in on:
                    pe.wait_ge(attnT_ready, i - 1)
                    reached(pe, expl_ready, i - 2)
                    project(ps_c[:, 256:512], attnT, wo_sb).then_inc(wo_done, 1)
                if "B" in on:
                    turn(i - 1, 1)
                    values(i - 1, 1 - p, 0)
                    scores(i - 1, 1 - p, 3)
                    turn(i - 1, 2)
                    values(i - 1, 1 - p, 1)
                if "A" in on:
                    pe.wait_ge(q_ready, i + 1)
                    alone(pe)
                    for src, off in ((q_rot, 0), (k_rot, 256)):
                        for gq in range(GROUPS):
                            for b in range(2):
                                r = slice(b * SEQ, (b + 1) * SEQ)
                                m = mm(ps_q[r, off + gq * SEQ:off + (gq + 1) * SEQ], src[r, gq * SEQ:(gq + 1) * SEQ],
                                       const[r, C_ID + b * SEQ:C_ID + (b + 1) * SEQ])
                    m.then_inc(qkT_done, 1)
                if "C" in on:
                    pe.wait_ge(xh2_ready, i - 1)
                    two_transposes(ps_c[:, 0:256], xh2).then_inc(x2T_done, 1)
                if "B" in on:
                    turn(i - 1, 3)
                    values(i - 1, 1 - p, 2)
                if "C" in on:
                    pe.wait_ge(xh2T_ready, i - 1)
                    project(ps_c[:, 256:256 + EXPERTS], xh2T, gate_sb).then_inc(router_done, 1)
                if "B" in on:
                    values(i - 1, 1 - p, 3)

            pe.wait_ge(consts_in, 16 * 8)
            pe.wait_ge(consts_ready, 7)
            pe.wait_ge(dve_const, 7)
            pipeline(pe, step)

            pe.wait_ge(gu_in, 16 * 8)
            pe.wait_ge(slot_ready, TILES)

            def turn_block(b, u, rnd):
                gp, j, p = u // BG % 2, u % BG, u % 2
                if j == 0:
                    pe.wait_ge(xb_in[gp], (rnd + 1) * 16)
                reached(pe, xbT_ready, b - 1)
                two_transposes(pp_xT[p], xb[:, gp, j]).then_inc(xbT_done, 1)

            def gate_up_block(b, u, rnd):
                gp, j, p = u // BG % 2, u % BG, u % 2
                e = pe.value_load(xb[0:1, gp, j, COL_EXP:COL_EXP + 1].bitcast(I32), min_val=0, max_val=EXPERTS - 1)
                pe.wait_ge(xbT_ready, b + 1)
                reached(pe, hid_ready, b - 1)
                for c in range(2):
                    m = mm(pp_gu[p][:, 0:2 * INNER], xbT[:, p, c, :],
                           gu_sb[:, bass.ds(e, 1), c, :].rearrange("p e n -> p (e n)"), start=c == 0, stop=c == 1)
                m.then_inc(gu_done, 1)

            def turn_hidden(b, u, rnd):
                p = u % 2
                pe.wait_ge(hid_ready, b + 1)
                reached(pe, hidT_ready, b - 1)
                t.transpose(pp_hT[p][0:INNER, 0:P], hid[:, p, :], ident).then_inc(hT_done, 1)

            def down_block(b, u, rnd):
                j, p = u % BG, u % 2
                pe.wait_ge(hidT_ready, b + 1)
                pe.wait_ge(w2_in[j], (rnd * 2 + u // BG + 1) * 16)
                reached(pe, yb_ready, b - 1)
                mm(pp_y[p][:, 0:DIM], hidT[:, p, :], w2_sb[:, j, :]).then_inc(y_done, 1)

            beats2(pe, {0: turn_block, 1: gate_up_block, 2: turn_hidden, 3: down_block})



def beats2(eng, stages):
    U = 2 * BG

    def beat(rounds, u):
        for s in sorted(stages):
            if isinstance(rounds, int) and not 0 <= rounds * U + u - s < BLOCKS:
                continue
            stages[s](rounds * U + (u - s), (u - s) % U, rounds + (u - s) // U)

    for u in range(U):
        beat(0, u)
    with eng.Fori(1, BLOCKS // U) as rounds:
        for u in range(U):
            beat(rounds, u)
    for u in range(max(stages)):
        beat(BLOCKS // U, u)


CHAIN_FULL = 29


def kernel(x, ctx_1024, fside_BxSx2_0, L0_xattn_Wq, L0_xattn_Wkv, L0_xattn_Wout, L0_xattn_bout,
           L0_ffn_gate_weight, L0_ffn_gate_up_proj, L0_ffn_down_proj):
    import concourse.bacc as bacc
    from concourse.bass_utils import run_bass_kernel_spmd

    def lay(a):
        return np.ascontiguousarray(a)

    def chunks(w):
        return lay(np.asarray(w).reshape(2, P, -1).transpose(1, 0, 2))

    wkv = np.asarray(L0_xattn_Wkv)
    const = np.zeros((P, C_END), np.float32)
    const[:, C_ID:C_ID + P] = np.eye(P)
    const[:, C_HM:C_HM + HG] = (np.arange(P)[:, None] % SEQ) // HD == np.arange(HG)
    const[:, C_IOTA:C_IOTA + EXPERTS] = np.arange(EXPERTS)
    const[:, C_DEST:C_DEST + TOPK] = np.arange(P)[:, None] * KSLOTS + np.arange(TOPK)
    const[:, C_TRI:C_TRI + P] = np.arange(P)[:, None] < np.arange(P)
    blank = np.zeros((P, ROW), np.int32)
    blank[:, COL_DEST] = 1 << 20
    arrays = {
        "x": lay(np.asarray(x).reshape(TOKENS, DIM)),
        "ctxT": lay(np.asarray(ctx_1024).reshape(TOKENS, CTX).T),
        "pos": lay(np.asarray(fside_BxSx2_0).reshape(TOKENS, 2)),
        "wq": chunks(L0_xattn_Wq),
        "wk": lay(wkv[:, :DIM]),
        "wv": lay(wkv[:, DIM:].reshape(CTX, PAIRS, 2, HD).transpose(0, 2, 1, 3).reshape(CTX, 2, DIM // 2)),
        "wo": chunks(L0_xattn_Wout),
        "bout": lay(np.broadcast_to(np.asarray(L0_xattn_bout), (P, DIM))),
        "gate": chunks(np.asarray(L0_ffn_gate_weight).T),
        "gu": lay(np.asarray(L0_ffn_gate_up_proj).transpose(2, 0, 1).reshape(2, P, EXPERTS, 2 * INNER).transpose(1, 2, 0, 3)),
        "w2": lay(np.asarray(L0_ffn_down_proj).transpose(0, 2, 1)),
        "const": const,
        "blank": blank.view(np.float32),
    }
    nc = bacc.Bacc("TRN2", target_bir_lowering=False, num_devices=1)
    aps = [nc.dram_tensor(f"in_{n}", a.shape, mybir.dt.from_np(a.dtype), kind="ExternalInput").ap() for n, a in arrays.items()]
    out = nc.dram_tensor("out", [TOKENS, DIM], F32, kind="ExternalOutput").ap()
    build(nc, *aps, out)
    r = run_bass_kernel_spmd(nc, [{f"in_{n}": a for n, a in arrays.items()}], core_ids=[0])
    return r.results[0]["out"].reshape(BATCH, SEQ, DIM)
```

```python
import math

import numpy as np

import concourse.bass as bass
from concourse import mybir
from contextlib import ExitStack

F32 = mybir.dt.float32
BF16 = mybir.dt.bfloat16
I32 = mybir.dt.int32
U32 = mybir.dt.uint32
ALU = mybir.AluOpType
ACT = mybir.ActivationFunctionType
AX = mybir.AxisListType

P = 128
BATCH, SEQ, DIM, CTX = 32, 64, 256, 128
HEADS, HD = 32, 8
EXPERTS, INNER, TOPK = 64, 96, 4
TOKENS = BATCH * SEQ
TILES = TOKENS // P
GROUPS = 4
HG = HEADS // GROUPS
PAIRS = HEADS // 2
PPG = PAIRS // GROUPS
EPS = 1e-5
SCALE = 1.0 / math.sqrt(HD)
TWO_PI = 2.0 * math.pi

ROW = DIM + 4
COL_DEST, COL_W, COL_EXP = DIM, DIM + 1, DIM + 2
BLOCKS = TOKENS * TOPK // P + EXPERTS
KSLOTS = TOPK + 1
BG = 2
NG = 8
ROUND = BG * NG
NB = 8

C_ID, C_HM, C_IOTA, C_DEST, C_TRI, C_END = 0, 128, 136, 200, 204, 332


class Chain:

    def __init__(self, eng, sem, base=0):
        self.eng, self.sem, self.base, self.n = eng, sem, base, 0

    def after(self, instruction):
        self.n += 1
        instruction.then_inc(self.sem, 1)

    def sync(self):
        self.eng.wait_ge(self.sem, self.base + self.n)


def reached(eng, sem, value):
    if not isinstance(value, int) or value > 0:
        eng.wait_ge(sem, value)


def build(nc, x_d, ctxT_d, pos_d, wq_d, wk_d, wv_d, wo_d, bout_d, gate_d, gu_d, w2_d, const_d, blank_d, out_d):
    rows_d = nc.dram_tensor("rows_d", [BLOCKS * P, ROW], F32, kind="Internal").ap()
    res_d = nc.dram_tensor("res_d", [TOKENS * KSLOTS, DIM], F32, kind="Internal").ap()
    res_tok = res_d.rearrange("(t k) d -> t k d", k=KSLOTS)

    ctx = ExitStack()
    with ctx:
        def sb(name, shape, dt=F32):
            return ctx.enter_context(nc.sbuf_tensor(name, shape, dt))

        def sem(name):
            return ctx.enter_context(nc.semaphore(name))

        gu_sb = sb("gu_sb", [P, EXPERTS, 2, 2 * INNER])
        wq_sb = sb("wq_sb", [P, 2, DIM])
        wk_sb = sb("wk_sb", [P, DIM])
        wv_sb = sb("wv_sb", [P, 2, DIM // 2])
        wo_sb = sb("wo_sb", [P, 2, DIM])
        gate_sb = sb("gate_sb", [P, 2, EXPERTS])
        bout_sb = sb("bout_sb", [P, DIM])
        const = sb("const", [P, C_END])
        blank = sb("blank", [P, ROW])
        ident = const[:, C_ID:C_ID + P]
        hmask = const[:, C_HM:C_HM + HG]
        iota_e = const[:, C_IOTA:C_IOTA + EXPERTS]
        tri = sb("tri", [P, P], BF16)
        ones_bf = sb("ones_bf", [P, P], BF16)
        ones_e = sb("ones_e", [P, EXPERTS])
        neg_half = sb("neg_half", [P, 1])

        pos_sb = sb("pos_sb", [P, TILES, 2])
        ang = sb("ang", [P, 2, TILES, 4])
        turns = sb("turns", [P, 2, TILES, 4])
        trig = sb("trig", [P, 2, TILES, 4])
        nsin = sb("nsin", [P, TILES, 4])

        xa = sb("xa", [P, 2, DIM])
        ctxT = sb("ctxT", [P, 2, P])
        st1 = sb("st1", [P, 6])
        mv1 = sb("mv1", [P, 2])
        ve1 = sb("ve1", [P, 1])
        rstd1 = sb("rstd1", [P, 1])
        xhat = sb("xhat", [P, DIM])
        xhT = sb("xhT", [P, 2, P])
        k_sb = sb("k_sb", [P, DIM])
        k_cos = sb("k_cos", [P, DIM])
        k_sin = sb("k_sin", [P, DIM])
        k_rot = sb("k_rot", [P, DIM])
        q_cos = sb("q_cos", [P, DIM])
        q_sin = sb("q_sin", [P, DIM])
        q_rot = sb("q_rot", [P, DIM])
        q_diag = sb("q_diag", [P, 2, GROUPS, P])
        k_mask = sb("k_mask", [P, 2, GROUPS, HG, SEQ])
        v_pair = sb("v_pair", [P, 2, 2, PAIRS, 2, HD + 1])

        mx = sb("mx", [P, 2, HG])
        shifted = sb("shifted", [P, 2, HG * SEQ])
        probT = sb("probT", [P, 2, PPG, P])

        rsum = sb("rsum", [P, HEADS])
        attn = sb("attn", [P, DIM])
        attnT = sb("attnT", [P, 2, P])
        xres = sb("xres", [P, 2, DIM])
        x2 = sb("x2", [P, 2, DIM])
        st2 = sb("st2", [P, 6])
        mv2 = sb("mv2", [P, 2])
        ve2 = sb("ve2", [P, 1])
        rstd2 = sb("rstd2", [P, 1])
        xh2 = sb("xh2", [P, DIM])
        xh2T = sb("xh2T", [P, 2, P])
        nmx = sb("nmx", [P, 1])
        expl = sb("expl", [P, EXPERTS])
        esum = sb("esum", [P, 1])
        resum = sb("resum", [P, 1])
        probs = sb("probs", [P, EXPERTS])
        top8 = sb("top8", [P, 8])
        idx8 = sb("idx8", [P, 8], U32)
        idxf = sb("idxf", [P, TOPK])
        wsum = sb("wsum", [P, 1])
        wclip = sb("wclip", [P, 1])
        rwsum = sb("rwsum", [P, 1])
        chosen = sb("chosen", [P, 2, TOPK, EXPERTS])
        taken = sb("taken", [P, 2, EXPERTS], BF16)
        rows = sb("rows", [P, 2, TOPK, ROW])

        count = sb("count", [P, EXPERTS])
        room = sb("room", [P, EXPERTS])
        base = sb("base", [P, EXPERTS])
        nblocks = sb("nblocks", [P, 1])
        rank = sb("rank", [P, EXPERTS])
        opens = sb("opens", [P, EXPERTS])
        upto = sb("upto", [P, EXPERTS])
        newest = sb("newest", [P, EXPERTS])
        fresh = sb("fresh", [P, EXPERTS])
        step_b = sb("step_b", [P, EXPERTS])
        spill = sb("spill", [P, EXPERTS])
        spill_b = sb("spill_b", [P, EXPERTS])
        open_b = sb("open_b", [P, EXPERTS])
        room_next = sb("room_next", [P, EXPERTS])
        slot_e = sb("slot_e", [P, EXPERTS])
        slot_r = sb("slot_r", [P, EXPERTS])
        slot_ke = sb("slot_ke", [P, TOPK, EXPERTS])
        slot_k = sb("slot_k", [P, TOPK])
        slot_i = sb("slot_i", [P, 2, TOPK], I32)
        dest = sb("dest", [P, TOPK])

        xb = sb("xb", [P, NG, BG, ROW])
        spare = k_mask[:].rearrange("p s g h k -> p (s g h k)").rearrange("p (x n d) -> p x n d", n=NB, d=DIM)
        w2_sb, yb = spare[0:INNER, 0], spare[:, 1]
        xbT = sb("xbT", [P, 2, 2, P])
        silu = sb("silu", [P, 2, INNER])
        hid = sb("hid", [P, 2, INNER])
        hidT = sb("hidT", [INNER, 2, P])

        NRES = 4
        gu_flat = gu_sb[:].rearrange("p e c n -> p (e c n)")
        res_cols = NRES * KSLOTS * DIM
        res = gu_flat[:, 0:res_cols].rearrange("p (j k d) -> p j k d", j=NRES, k=KSLOTS)
        fin = gu_flat[:, res_cols:res_cols + NRES * DIM].rearrange("p (j d) -> p j d", j=NRES)

        bank = [ctx.enter_context(nc.psum_tensor(f"bank{i}", [P, 512], F32)) for i in range(8)]
        ps_q, ps_kv, ps_o, ps_c = bank[0], bank[1], bank[6], bank[7]
        ps_s, ps_t = bank[2:4], bank[4:6]
        o_view = ps_o[:, 0:PAIRS * 2 * (HD + 1)].rearrange("p (h d) -> p h d", d=HD + 1)
        RANK = 320
        pp_xT, pp_gu, pp_hT, pp_y = bank[0:2], bank[2:4], bank[4:6], bank[6:8]

        consts_in = sem("consts_in"); pos_in = sem("pos_in")
        consts_ready = sem("consts_ready"); dve_const = sem("dve_const")
        angles_ready = sem("angles_ready"); trig_ready = sem("trig_ready"); nsin_ready = sem("nsin_ready")
        blank_rows = sem("blank_rows")
        gu_in = sem("gu_in")
        xa_in = [sem(f"xa_in{p}") for p in range(2)]
        xres_in = [sem(f"xres_in{p}") for p in range(2)]
        var1_ready = sem("var1_ready"); rstd1_ready = sem("rstd1_ready"); xhat_ready = sem("xhat_ready")
        xT_done = sem("xT_done"); xhT_ready = sem("xhT_ready")
        kv_done = sem("kv_done"); q_done = sem("q_done")
        k_in = sem("k_in"); kparts_ready = sem("kparts_ready"); qparts_ready = sem("qparts_ready")
        k_ready = sem("k_ready"); q_ready = sem("q_ready")
        qkT_done = sem("qkT_done")
        qdiag_ready = sem("qdiag_ready"); kmask_ready = sem("kmask_ready"); v_ready = sem("v_ready")
        s_done = sem("s_done"); max_ready = sem("max_ready"); shifted_ready = sem("shifted_ready")
        t_done = sem("t_done"); prob_ready = sem("prob_ready"); av_done = sem("av_done")
        rsum_ready = sem("rsum_ready"); attn_ready = sem("attn_ready")
        aT_done = sem("aT_done"); attnT_ready = sem("attnT_ready"); wo_done = sem("wo_done")
        xres_ready = sem("xres_ready"); x2_ready = sem("x2_ready")
        x2_stored = [sem(f"x2_stored{p}") for p in range(2)]
        var2_ready = sem("var2_ready"); rstd2_ready = sem("rstd2_ready"); xh2_ready = sem("xh2_ready")
        x2T_done = sem("x2T_done"); xh2T_ready = sem("xh2T_ready"); router_done = sem("router_done")
        nmx_ready = sem("nmx_ready"); expl_ready = sem("expl_ready")
        taken_ready = sem("taken_ready"); rank_done = sem("rank_done"); rank_read = sem("rank_read"); slot_ready = sem("slot_ready")
        rowvals_ready = sem("rowvals_ready")
        scattered = [sem(f"scattered{p}") for p in range(2)]
        dve_step = sem("dve_step")
        passed = sem("passed")
        xb_in = [sem(f"xb_in{n}") for n in range(NG)]
        w2_in = [sem(f"w2_in{n}") for n in range(NB)]
        xbT_done = sem("xbT_done"); xbT_ready = sem("xbT_ready"); gu_done = sem("gu_done")
        silu_ready = sem("silu_ready"); hid_ready = sem("hid_ready"); hT_done = sem("hT_done")
        hidT_ready = sem("hidT_ready"); y_done = sem("y_done"); yb_ready = sem("yb_ready")
        y_scattered = [sem(f"y_scattered{n}") for n in range(NB)]
        res_in = [sem(f"res_in{j}") for j in range(NRES)]
        fin_ready = sem("fin_ready")
        fin_out = [sem(f"fin_out{j}") for j in range(NRES)]

        def factors(i):
            cos = trig[:, 1, bass.ds(i, 1), :].unsqueeze(3).to_broadcast([P, HEADS, 4, 2])
            return (cos, nsin[:, bass.ds(i, 1), :].to_broadcast([P, HEADS, 4]),
                    trig[:, 0, bass.ds(i, 1), :].to_broadcast([P, HEADS, 4]))

        def alone(eng):
            eng.sem_inc(passed, 1)

        INIT = BLOCKS // 8
        GU_STEP = EXPERTS // (TILES - 6)
        GU_REST = EXPERTS - GU_STEP * (TILES - 6)

        def pipeline(eng, step):
            def stages(i):
                on = set()
                if i + 1 < TILES:
                    on.add("L")
                for lag, name in enumerate("ABCDE"):
                    if 0 <= i - lag < TILES:
                        on.add(name)
                return on

            for i in range(4):
                step(i, i % 2, i // 2, stages(i))
            with eng.Fori(2, TILES // 2 - 1) as twos:
                i = twos * 2
                step(i, 0, twos, set("LABCDE"))
                step(i + 1, 1, twos, set("LABCDE"))
            for i in range(TILES - 2, TILES + 4):
                step(i, i % 2, i // 2, stages(i))

        def earlier(twos, p, lag):
            return twos + (p - lag) // 2

        block = ctx.enter_context(nc.Block())

        @block.sync
        def _(sp):
            sp.dma_start(pos_sb[:], pos_d.rearrange("(t p) a -> p t a", p=P)).then_inc(pos_in, 16)
            sp.dma_start(const[:], const_d).then_inc(consts_in, 16)
            sp.dma_start(blank[:], blank_d).then_inc(consts_in, 16)
            sp.dma_start(wk_sb[:], wk_d).then_inc(consts_in, 16)
            sp.dma_start(wv_sb[:], wv_d).then_inc(consts_in, 16)
            sp.dma_start(wq_sb[:], wq_d).then_inc(consts_in, 16)
            sp.dma_start(wo_sb[:], wo_d).then_inc(consts_in, 16)
            sp.dma_start(gate_sb[:], gate_d).then_inc(consts_in, 16)
            sp.dma_start(bout_sb[:], bout_d).then_inc(consts_in, 16)

            def load_tile(i, p):
                reached(sp, xhat_ready, i - 1)
                reached(sp, kv_done, i - 1)
                sp.dma_start(xa[:, p, :], x_d[bass.ds(i * P, P), :]).then_inc(xa_in[p], 16)
                sp.dma_start(ctxT[:, p, :], ctxT_d[:, bass.ds(i * P, P)]).then_inc(xa_in[p], 16)

            def load_residual(i, p):
                reached(sp, x2_ready, i - 1)
                sp.dma_start(xres[:, p, :], x_d[bass.ds(i * P, P), :]).then_inc(xres_in[p], 16)

            load_tile(0, 0)
            load_tile(1, 1)
            load_residual(0, 0)
            load_residual(1, 1)
            sp.wait_ge(consts_in, 16 * 8)
            view = rows_d.rearrange("(b p) c -> p b c", p=P)

            def blank_part(k):
                sp.dma_start(view[:, k * INIT:(k + 1) * INIT, :],
                             blank[:].unsqueeze(1).to_broadcast([P, INIT, ROW])).then_inc(blank_rows, 16)

            blank_part(0)
            blank_part(1)

            def store_x2(i, p):
                sp.wait_ge(x2_ready, i + 1)
                sp.dma_start(res_tok[bass.ds(i * P, P), TOPK, :], x2[:, p, :]).then_inc(x2_stored[p], 16)

            def step(i, p, twos, on):
                if isinstance(i, int) is False or i + 2 < TILES:
                    load_tile(i + 2, p)
                if "C" in on:
                    store_x2(i - 2, p)
                    if isinstance(i, int) is False or i < TILES:
                        load_residual(i, p)

            def load_gate_up(e, n):
                sp.dma_start(gu_sb[:, bass.ds(e, n)], gu_d[:, bass.ds(e, n)]).then_inc(gu_in, 16)

            for i in range(4):
                step(i, i % 2, i // 2, {"C"} if i >= 2 else set())
                if i < 3:
                    blank_part(2 * i + 2)
                    blank_part(2 * i + 3)
                else:
                    load_gate_up(EXPERTS - GU_REST, GU_REST)
            with sp.Fori(2, TILES // 2 - 1) as twos:
                i = twos * 2
                step(i, 0, twos, {"C"})
                load_gate_up((i - 4) * GU_STEP, GU_STEP)
                step(i + 1, 1, twos, {"C"})
                load_gate_up((i - 3) * GU_STEP, GU_STEP)
            for i in range(TILES - 2, TILES + 2):
                step(i, i % 2, i // 2, {"C"})

            for p in range(2):
                sp.wait_ge(scattered[p], 16 * TOPK * TILES // 2)

            loads = rows_d.rearrange("(g j p) c -> g p j c", p=P, j=BG)

            def load_rows(rnd, n):
                if not isinstance(rnd, int) or rnd > 0:
                    for j in range(BG):
                        u = n * BG + j
                        sp.wait_ge(y_scattered[u % NB], ((rnd - 1) * (ROUND // NB) + u // NB + 1) * 16)
                sp.dma_start(xb[:, n], loads[bass.ds(rnd * NG + n, 1)].rearrange("g p j c -> (g p) j c")).then_inc(xb_in[n], 16)

            def load_down(rnd, n):
                sp.wait_ge(xb_in[n], (rnd + 1) * 16)
                alone(sp)
                for j in range(BG):
                    u = n * BG + j
                    e = sp.value_load(xb[0:1, n, j, COL_EXP:COL_EXP + 1].bitcast(I32), min_val=0, max_val=EXPERTS - 1)
                    reached(sp, y_done, rnd * ROUND + (u - NB + 1))
                    sp.dma_start(w2_sb[:, u % NB, :], w2_d[bass.ds(e, 1)].rearrange("e i d -> (e i) d")).then_inc(w2_in[u % NB], 16)

            AHEAD = 2
            for n in range(AHEAD):
                load_rows(0, n)
            for n in range(NG - AHEAD):
                load_rows(0, n + AHEAD)
                load_down(0, n)
            with sp.Fori(1, BLOCKS // ROUND) as rnd:
                for n in range(NG):
                    load_rows(rnd, n)
                    if n < AHEAD:
                        load_down(rnd - 1, n + NG - AHEAD)
                    else:
                        load_down(rnd, n - AHEAD)
            for n in range(NG - AHEAD, NG):
                load_down(BLOCKS // ROUND - 1, n)

            for n in range(NB):
                sp.wait_ge(y_scattered[n], BLOCKS // NB * 16)
            for p in range(2):
                sp.wait_ge(x2_stored[p], 16 * TILES // 2)

            def load_results(i, j):
                reached(sp, fin_ready, i - NRES + 1)
                sp.dma_start(res[:, j], res_tok[bass.ds(i * P, P)]).then_inc(res_in[j], 16)

            for j in range(NRES):
                load_results(j, j)
            with sp.Fori(1, TILES // NRES) as fours:
                i = fours * NRES
                for j in range(NRES):
                    load_results(i + j, j)

        @block.gpsimd
        def _(pool):
            g = nc.gpsimd
            g.memset(neg_half[:], -0.5).then_inc(consts_ready, 1)
            g.memset(ones_e[:], 1.0).then_inc(consts_ready, 1)
            g.memset(ones_bf[:], 1.0).then_inc(consts_ready, 1)
            g.memset(q_diag[:], 0.0).then_inc(consts_ready, 1)
            g.memset(v_pair[:], 0.0).then_inc(consts_ready, 1)
            pool.wait_ge(consts_ready, 5)
            for h in range(2):
                r = slice(h * SEQ, (h + 1) * SEQ)
                g.memset(v_pair[r, :, :, :, h, HD:HD + 1].rearrange("p s b n o -> p (s b n) o"), 1.0).then_inc(consts_ready, 1)

            def rstd(var, out, ready, n, done):
                pool.wait_ge(ready, n)
                g.tensor_tensor(out[:], var[:], neg_half[:], ALU.pow).then_inc(done, 1)

            def step(i, p, twos, on):
                if "E" in on:
                    pool.wait_ge(rowvals_ready, i - 3)
                    alone(pool)
                    pool.wait_ge(slot_ready, i - 3)
                    alone(pool)
                    for k in range(TOPK):
                        g.indirect_dma_start(rows_d, bass.IndirectOffsetOnAxis(ap=slot_i[:, p, k:k + 1], axis=0),
                                             rows[:, p, k, :], None).then_inc(scattered[p], 16)
                if "A" in on:
                    pool.wait_ge(k_in, i + 1)
                    reached(pool, qkT_done, i)
                    s = k_sb[:].rearrange("p (h c two) -> p h c two", c=4, two=2)
                    os_ = k_sin[:].rearrange("p (h c two) -> p h c two", c=4, two=2)
                    cos, sin_e, sin_o = factors(i)
                    g.tensor_tensor(k_cos[:].rearrange("p (h c two) -> p h c two", c=4, two=2), s, cos, ALU.mult)
                    g.tensor_tensor(os_[:, :, :, 0], s[:, :, :, 1], sin_e, ALU.mult)
                    g.tensor_tensor(os_[:, :, :, 1], s[:, :, :, 0], sin_o, ALU.mult).then_inc(kparts_ready, 1)
                    pool.wait_ge(kparts_ready, i + 1)
                    g.tensor_tensor(k_rot[:], k_cos[:], k_sin[:], ALU.add).then_inc(k_ready, 1)
                    pool.wait_ge(qparts_ready, i + 1)
                    g.tensor_tensor(q_rot[:], q_cos[:], q_sin[:], ALU.add).then_inc(q_ready, 1)
                if "C" in on:
                    rstd(ve2, rstd2, var2_ready, i - 1, rstd2_ready)
                if "L" in on:
                    rstd(ve1, rstd1, var1_ready, i + 2, rstd1_ready)
                if isinstance(i, int) and i == 3:
                    pool.wait_ge(blank_rows, 16 * 8)
                if "B" in on:
                    pool.wait_ge(xres_in[1 - p], 16 * (earlier(twos, p, 1) + 1))
                    g.tensor_tensor(xres[:, 1 - p, :], xres[:, 1 - p, :], bout_sb[:], ALU.add).then_inc(xres_ready, 1)

            pool.wait_ge(consts_in, 16 * 8)
            rstd(ve1, rstd1, var1_ready, 1, rstd1_ready)
            pool.wait_ge(dve_const, 7)
            pipeline(pool, step)

            with pool.Fori(0, BLOCKS // ROUND) as rnd:
                for u in range(ROUND):
                    pool.wait_ge(yb_ready, rnd * ROUND + (u + 1))
                    alone(pool)
                    g.indirect_dma_start(
                        res_d, bass.IndirectOffsetOnAxis(ap=xb[:, u // BG, u % BG, COL_DEST:COL_DEST + 1].bitcast(I32), axis=0),
                        yb[:, u % NB, :], None, bounds_check=TOKENS * KSLOTS - 1, oob_is_err=False).then_inc(y_scattered[u % NB], 16)

        @block.scalar
        def _(act):
            a = nc.scalar
            act.wait_ge(angles_ready, 1)
            a.activation(trig[:], ang[:], ACT.Sin).then_inc(trig_ready, 1)

            def kmask_part(i, p, hs):
                for h in hs:
                    m = a.activation(k_mask[:, p, :, h, :], ps_q[:, 256:512].rearrange("p (g k) -> p g k", g=GROUPS),
                                     ACT.Copy, scale=hmask[:, h:h + 1])
                return m

            def exp_group(i, g):
                n = i * GROUPS + g
                act.wait_ge(t_done, n + 1)
                reached(act, av_done, n - 1)
                a.activation(probT[:, g % 2].rearrange("p j q -> p (j q)"), ps_t[g % 2][:], ACT.Exp,
                             scale=SCALE).then_inc(prob_ready, 1)

            def step(i, p, twos, on):
                if "A" in on:
                    act.wait_ge(xT_done, i + 1)
                    reached(act, q_done, i)
                    a.copy(xhT[:].rearrange("p c t -> p (c t)"), ps_q[:, 0:256]).then_inc(xhT_ready, 1)
                if "C" in on:
                    act.wait_ge(aT_done, i - 1)
                    reached(act, wo_done, i - 2)
                    a.copy(attnT[:].rearrange("p c t -> p (c t)"), ps_c[:, 0:256]).then_inc(attnT_ready, 1)
                if "A" in on:
                    act.wait_ge(kv_done, i + 1)
                    reached(act, kparts_ready, i)
                    a.copy(k_sb[:], ps_kv[:, 0:256]).then_inc(k_in, 1)
                    if not isinstance(i, int) or i >= 2:
                        act.wait_ge(av_done, GROUPS * (i - 1))
                    for h in range(2):
                        r = slice(h * SEQ, (h + 1) * SEQ)
                        m = a.copy(v_pair[r, p, :, :, h, 0:HD],
                                   ps_kv[r, 256:512].rearrange("p (b n d) -> p b n d", b=2, d=HD))
                    m.then_inc(v_ready, 1)
                if "B" in on:
                    exp_group(i - 1, 0)
                    exp_group(i - 1, 1)
                    exp_group(i - 1, 2)
                if "A" in on:
                    act.wait_ge(qkT_done, i + 1)
                    if not isinstance(i, int) or i >= 2:
                        act.wait_ge(s_done, GROUPS * (i - 1))
                    for b in range(2):
                        r = slice(b * SEQ, (b + 1) * SEQ)
                        m = a.copy(q_diag[r, p, :, r], ps_q[r, 0:256].rearrange("p (g q) -> p g q", g=GROUPS))
                    m.then_inc(qdiag_ready, 1)
                    kmask_part(i, p, range(0, 3))
                if "C" in on:
                    act.wait_ge(x2T_done, i - 1)
                    reached(act, router_done, i - 2)
                    a.copy(xh2T[:].rearrange("p c t -> p (c t)"), ps_c[:, 0:256]).then_inc(xh2T_ready, 1)
                if "B" in on:
                    exp_group(i - 1, 3)
                if "A" in on:
                    kmask_part(i, p, range(3, HG)).then_inc(kmask_ready, 1)
                if "C" in on:
                    if not isinstance(i, int) or i >= 4:
                        act.wait_ge(scattered[p], 16 * TOPK * earlier(twos, p, 2))
                    act.wait_ge(nmx_ready, i - 1)
                    a.activation(expl[:], ps_c[:, 256:256 + EXPERTS], ACT.Exp, bias=nmx[:, 0:1],
                                 accum_out=esum[:, 0:1]).then_inc(expl_ready, 1)
                    for k in range(TOPK):
                        m = a.copy(rows[:, p, k, 0:DIM], xh2[:])
                    m.then_inc(rowvals_ready, 1)

            act.wait_ge(consts_in, 16 * 8)
            act.wait_ge(consts_ready, 7)
            pipeline(act, step)

            def silu_block(b, u, rnd):
                p = u % 2
                act.wait_ge(gu_done, b + 1)
                reached(act, hid_ready, b - 1)
                a.activation(silu[:, p, :], pp_gu[p][:, 0:INNER], ACT.Silu).then_inc(silu_ready, 1)

            def hidT_block(b, u, rnd):
                p = u % 2
                act.wait_ge(hT_done, b + 1)
                reached(act, y_done, b - 1)
                a.copy(hidT[:, p, :], pp_hT[p][0:INNER, 0:P]).then_inc(hidT_ready, 1)

            def weigh_block(b, u, rnd):
                act.wait_ge(y_done, b + 1)
                reached(act, y_scattered[u % NB], (rnd * (ROUND // NB) + u // NB) * 16)
                a.activation(yb[:, u % NB, :], pp_y[u % 2][:, 0:DIM], ACT.Copy,
                             scale=xb[:, u // BG, u % BG, COL_W:COL_W + 1]).then_inc(yb_ready, 1)

            beats2(act, {1: silu_block, 2: hidT_block,
                         3: weigh_block})

            def store(i, j):
                act.wait_ge(fin_ready, i + 1)
                act.dma_start(out_d[bass.ds(i * P, P), :], fin[:, j, :]).then_inc(fin_out[j], 16)

            for j in range(NRES):
                store(j, j)
            with act.Fori(1, TILES // NRES) as fours:
                i = fours * NRES
                for j in range(NRES):
                    store(i + j, j)
            for j in range(NRES):
                act.wait_ge(fin_out[j], 16 * TILES // NRES)

        @block.vector
        def _(dve):
            v = nc.vector
            prep = Chain(dve, dve_const)

            def link(instruction):
                prep.after(instruction)
                prep.sync()

            dve.wait_ge(pos_in, 16)
            for axis in range(2):
                for f in range(2):
                    m = v.tensor_scalar(ang[:, 0, :, 2 * axis + f], pos_sb[:, :, axis], 10000.0 ** (-f / 2), None, ALU.mult)
            link(m)
            link(v.tensor_scalar(ang[:, 1], ang[:, 0], math.pi / 2, None, ALU.add))
            ROUND = 1.5 * 2.0 ** 23
            HI = 6.28125
            link(v.tensor_scalar(turns[:], ang[:], 1.0 / TWO_PI, ROUND, ALU.mult, ALU.add))
            link(v.tensor_scalar(turns[:], turns[:], ROUND, None, ALU.subtract))
            link(v.scalar_tensor_tensor(ang[:], turns[:], -HI, ang[:], ALU.mult, ALU.add))
            link(v.scalar_tensor_tensor(ang[:], turns[:], -(TWO_PI - HI), ang[:], ALU.mult, ALU.add))
            v.tensor_scalar(ang[:], ang[:], 3.1415925, -3.1415925, ALU.min, ALU.max).then_inc(angles_ready, 1)
            dve.wait_ge(consts_in, 16 * 8)
            v.tensor_copy(tri[:], const[:, C_TRI:C_TRI + P])
            v.tensor_copy(dest[:], const[:, C_DEST:C_DEST + TOPK])
            v.memset(count[:], 0.0)
            v.memset(room[:], 0.0)
            v.memset(base[:], 0.0)
            v.memset(nblocks[:], 0.0)
            v.memset(rows[:], 0.0)
            dve.wait_ge(trig_ready, 1)
            link(v.tensor_scalar(nsin[:], trig[:, 0], -1.0, None, ALU.mult))
            dve.wait_ge(consts_ready, 7)

            def rotate_q(i):
                s = ps_q[:, 256:512].rearrange("p (h c two) -> p h c two", c=4, two=2)
                os_ = q_sin[:].rearrange("p (h c two) -> p h c two", c=4, two=2)
                cos, sin_e, sin_o = factors(i)
                v.tensor_tensor(q_cos[:].rearrange("p (h c two) -> p h c two", c=4, two=2), s, cos, ALU.mult)
                v.tensor_tensor(os_[:, :, :, 0], s[:, :, :, 1], sin_e, ALU.mult)
                v.tensor_tensor(os_[:, :, :, 1], s[:, :, :, 0], sin_o, ALU.mult).then_inc(qparts_ready, 1)

            def scores_of(g):
                return ps_s[g % 2][:].rearrange("p (h k) -> p h k", h=HG)

            def group_max(i, g):
                dve.wait_ge(s_done, i * GROUPS + g + 1)
                v.tensor_reduce(mx[:, g % 2, :], scores_of(g), AX.X, ALU.max).then_inc(max_ready, 1)

            def group_shift(i, g):
                n = i * GROUPS + g
                dve.wait_ge(max_ready, n + 1)
                reached(dve, t_done, n - 1)
                v.tensor_tensor(shifted[:, g % 2, :].rearrange("p (h k) -> p h k", h=HG), scores_of(g),
                                mx[:, g % 2, :].unsqueeze(2).to_broadcast([P, HG, SEQ]),
                                ALU.subtract).then_inc(shifted_ready, 1)

            def step(i, p, twos, on, base_n):
                ch = Chain(dve, dve_step, base_n)

                def link(x):
                    ch.after(x)
                    ch.sync()

                A, B, C, D, L = (x in on for x in "ABCDL")
                q = 1 - p
                if C:
                    dve.wait_ge(av_done, GROUPS * (i - 1))
                    v.reciprocal(rsum[:], o_view[:, :, HD]).then_inc(rsum_ready, 1)
                if B:
                    group_max(i - 1, 0)
                if C:
                    dve.wait_ge(rsum_ready, i - 1)
                    reached(dve, aT_done, i - 2)
                    v.tensor_tensor(attn[:].rearrange("p (h d) -> p h d", d=HD), o_view[:, :, 0:HD],
                                    rsum[:].unsqueeze(2).to_broadcast([P, HEADS, HD]), ALU.mult).then_inc(attn_ready, 1)
                if B:
                    group_shift(i - 1, 0)
                    group_max(i - 1, 1)
                if D:
                    dve.wait_ge(rank_done, i - 2)
                    v.tensor_tensor(rank[:], ps_o[:, RANK:RANK + EXPERTS], count[:], ALU.add)
                    v.tensor_tensor(count[:], ps_o[:, RANK + EXPERTS:RANK + 2 * EXPERTS], count[:], ALU.add).then_inc(rank_read, 1)
                if B:
                    group_shift(i - 1, 1)
                if D:
                    dve.wait_ge(rank_read, i - 2)
                    v.tensor_tensor(spill[:], rank[:], room[:], ALU.is_ge)
                    ch.after(v.tensor_tensor(opens[:], count[:], room[:], ALU.is_gt))
                    ch.after(v.tensor_tensor(slot_e[:], rank[:], base[:], ALU.add))
                if A:
                    dve.wait_ge(q_done, i + 1)
                    reached(dve, q_ready, i)
                    rotate_q(i)
                if D:
                    ch.sync()
                    ch.after(v.tensor_tensor_scan(upto[:], ones_e[:], opens[:], nblocks[:, 0:1], ALU.mult, ALU.add))
                if B:
                    group_max(i - 1, 2)
                if D:
                    ch.sync()
                    ch.after(v.tensor_copy(nblocks[:], upto[:, EXPERTS - 1:EXPERTS]))
                    ch.after(v.tensor_tensor(newest[:], upto[:], opens[:], ALU.subtract))
                if B:
                    group_shift(i - 1, 2)
                if D:
                    ch.sync()
                    ch.after(v.scalar_tensor_tensor(fresh[:], newest[:], float(P), room[:], ALU.mult, ALU.subtract))
                if C:
                    dve.wait_ge(wo_done, i - 1)
                    dve.wait_ge(xres_ready, i - 1)
                    if not isinstance(i, int) or i >= 4:
                        dve.wait_ge(x2_stored[p], 16 * earlier(twos, p, 2))
                    v.tensor_tensor(x2[:, p, :], ps_c[:, 256:512], xres[:, p, :], ALU.add).then_inc(x2_ready, 1)
                if D:
                    ch.sync()
                    ch.after(v.tensor_tensor(step_b[:], fresh[:], base[:], ALU.subtract))
                    ch.after(v.scalar_tensor_tensor(room_next[:], opens[:], float(P), room[:], ALU.mult, ALU.add))
                if C:
                    dve.wait_ge(x2_ready, i - 1)
                    ch.after(v.bn_stats(st2[:], x2[:, p, :]))
                if D:
                    ch.sync()
                    ch.after(v.tensor_tensor(spill_b[:], spill[:], step_b[:], ALU.mult))
                    ch.after(v.tensor_tensor(open_b[:], step_b[:], opens[:], ALU.mult))
                    ch.after(v.tensor_copy(room[:], room_next[:]))
                if C:
                    ch.sync()
                    alone(dve)
                    ch.after(v.bn_aggr(mv2[:], st2[:]))
                if B:
                    group_max(i - 1, 3)
                if C:
                    ch.sync()
                    v.tensor_scalar(ve2[:], mv2[:, 1:2], EPS, None, ALU.add).then_inc(var2_ready, 1)
                if D:
                    ch.sync()
                    ch.after(v.tensor_tensor(slot_r[:], slot_e[:], spill_b[:], ALU.add))
                    ch.after(v.tensor_tensor(base[:], base[:], open_b[:], ALU.add))
                if B:
                    group_shift(i - 1, 3)
                if L:
                    dve.wait_ge(xa_in[q], 32 * (earlier(twos, p, -1) + 1))
                    ch.after(v.bn_stats(st1[:], xa[:, q, :]))
                if D:
                    ch.sync()
                    ch.after(v.tensor_tensor(slot_ke[:], chosen[:, q], slot_r[:].unsqueeze(1).to_broadcast([P, TOPK, EXPERTS]), ALU.mult))
                if L:
                    ch.sync()
                    alone(dve)
                    ch.after(v.bn_aggr(mv1[:], st1[:]))
                if C:
                    dve.wait_ge(rstd2_ready, i - 1)
                    reached(dve, rowvals_ready, i - 2)
                    reached(dve, x2T_done, i - 2)
                    v.tensor_scalar(xh2[:], x2[:, p, :], mv2[:, 0:1], rstd2[:, 0:1], ALU.subtract, ALU.mult).then_inc(xh2_ready, 1)
                if L:
                    ch.sync()
                    v.tensor_scalar(ve1[:], mv1[:, 1:2], EPS, None, ALU.add).then_inc(var1_ready, 1)
                if D:
                    ch.sync()
                    link(v.tensor_reduce(slot_k[:], slot_ke[:], AX.X, ALU.add))
                    if not isinstance(i, int) or i >= 5:
                        dve.wait_ge(scattered[q], 16 * TOPK * earlier(twos, p, 3))
                    v.tensor_copy(slot_i[:, q, :], slot_k[:]).then_inc(slot_ready, 1)
                if C:
                    dve.wait_ge(router_done, i - 1)
                    v.tensor_reduce(nmx[:], ps_c[:, 256:256 + EXPERTS], AX.X, ALU.max, negate=True).then_inc(nmx_ready, 1)
                if L:
                    dve.wait_ge(rstd1_ready, i + 2)
                    reached(dve, xT_done, i + 1)
                    v.tensor_scalar(xhat[:], xa[:, q, :], mv1[:, 0:1], rstd1[:, 0:1], ALU.subtract, ALU.mult).then_inc(xhat_ready, 1)
                if C:
                    dve.wait_ge(expl_ready, i - 1)
                    link(v.reciprocal(resum[:], esum[:]))
                    link(v.tensor_scalar(probs[:], expl[:], resum[:, 0:1], None, ALU.mult))
                    alone(dve)
                    link(v.max(top8[:], probs[:]))
                    alone(dve)
                    ch.after(v.max_index(idx8[:], top8[:], probs[:]))
                    link(v.tensor_reduce(wsum[:], top8[:, 0:TOPK], AX.X, ALU.add))
                    ch.after(v.tensor_copy(idxf[:], idx8[:, 0:TOPK]))
                    link(v.tensor_scalar(wclip[:], wsum[:], 1e-12, None, ALU.max))
                    ch.after(v.tensor_tensor(chosen[:, p], iota_e.unsqueeze(1).to_broadcast([P, TOPK, EXPERTS]),
                                             idxf[:].unsqueeze(2).to_broadcast([P, TOPK, EXPERTS]), ALU.is_equal))
                    link(v.reciprocal(rwsum[:], wclip[:]))
                    with nc.allow_low_precision(reason="zeros and ones"):
                        v.tensor_reduce(taken[:, p, :], chosen[:, p].rearrange("p k e -> p e k"), AX.X, ALU.add).then_inc(taken_ready, 1)
                    dve.wait_ge(rowvals_ready, i - 1)
                    v.tensor_scalar(rows[:, p, :, COL_W], top8[:, 0:TOPK], rwsum[:, 0:1], None, ALU.mult)
                    v.tensor_copy(rows[:, p, :, COL_EXP].bitcast(I32), idx8[:, 0:TOPK])
                    link(v.tensor_copy(rows[:, p, :, COL_DEST].bitcast(I32), dest[:]))
                    ch.after(v.tensor_scalar(dest[:], dest[:], float(P * KSLOTS), None, ALU.add))
                return ch.n

            total = 0
            first = Chain(dve, dve_step, 0)
            dve.wait_ge(xa_in[0], 32)
            first.after(v.bn_stats(st1[:], xa[:, 0, :]))
            first.sync()
            first.after(v.bn_aggr(mv1[:], st1[:]))
            first.sync()
            v.tensor_scalar(ve1[:], mv1[:, 1:2], EPS, None, ALU.add).then_inc(var1_ready, 1)
            dve.wait_ge(rstd1_ready, 1)
            v.tensor_scalar(xhat[:], xa[:, 0, :], mv1[:, 0:1], rstd1[:, 0:1], ALU.subtract, ALU.mult).then_inc(xhat_ready, 1)
            total = first.n

            def stages(i):
                on = set("L") if i + 1 < TILES else set()
                return on | {s for lag, s in enumerate("ABCD") if 0 <= i - lag < TILES}

            for i in range(4):
                total += step(i, i % 2, i // 2, stages(i), total)
            start = total
            FULL = CHAIN_FULL
            with dve.Fori(2, TILES // 2 - 1) as twos:
                i = twos * 2
                b0 = twos * (2 * FULL) + (start - 4 * FULL)
                n = step(i, 0, twos, set("LABCDE"), b0)
                n2 = step(i + 1, 1, twos, set("LABCDE"), b0 + FULL)
                assert n == FULL and n2 == FULL, (n, n2)
            total = start + FULL * (TILES - 6)
            for i in range(TILES - 2, TILES + 3):
                total += step(i, i % 2, i // 2, stages(i), total)

            def xbT_block(b, u, rnd):
                p = u % 2
                dve.wait_ge(xbT_done, b + 1)
                reached(dve, gu_done, b - 1)
                v.tensor_copy(xbT[:, p].rearrange("p c t -> p (c t)"), pp_xT[p][:, 0:DIM]).then_inc(xbT_ready, 1)

            def hid_block(b, u, rnd):
                p = u % 2
                dve.wait_ge(silu_ready, b + 1)
                reached(dve, hT_done, b - 1)
                v.tensor_tensor(hid[:, p, :], pp_gu[p][:, INNER:2 * INNER], silu[:, p, :], ALU.mult).then_inc(hid_ready, 1)

            beats2(dve, {0: xbT_block, 1: hid_block})

            def finish(i, j, k):
                dve.wait_ge(res_in[j], (k + 1) * 16)
                if not isinstance(i, int):
                    dve.wait_ge(fin_out[j], k * 16)
                v.tensor_reduce(fin[:, j, :], res[:, j].rearrange("p k d -> p d k"), AX.X, ALU.add).then_inc(fin_ready, 1)

            for j in range(NRES):
                finish(j, j, 0)
            with dve.Fori(1, TILES // NRES) as fours:
                i = fours * NRES
                for j in range(NRES):
                    finish(i + j, j, fours)

        @block.tensor
        def _(pe):
            t = nc.tensor

            def mm(out, lhsT, rhs, start=True, stop=True):
                return t.matmul(out, lhsT, rhs, start=start, stop=stop)

            def two_transposes(ps, src):
                for c in range(2):
                    m = t.transpose(ps[:, c * P:(c + 1) * P], src[:, c * P:(c + 1) * P], ident)
                return m

            def project(ps, lhsT, w):
                for c in range(2):
                    m = mm(ps, lhsT[:, c, :], w[:, c, :], start=c == 0, stop=c == 1)
                return m

            def scores(i, p, g):
                n = i * GROUPS + g
                if g == 0:
                    pe.wait_ge(qdiag_ready, i + 1)
                    pe.wait_ge(kmask_ready, i + 1)
                reached(pe, shifted_ready, n - 1)
                mm(ps_s[g % 2][:], q_diag[:, p, g, :], k_mask[:, p, g].rearrange("p h k -> p (h k)")).then_inc(s_done, 1)

            def turn(i, g):
                n = i * GROUPS + g
                pe.wait_ge(shifted_ready, n + 1)
                reached(pe, prob_ready, n - 1)
                for j in range(PPG):
                    m = t.transpose(ps_t[g % 2][:, j * P:(j + 1) * P], shifted[:, g % 2, j * P:(j + 1) * P], ident)
                m.then_inc(t_done, 1)

            def values(i, p, g):
                n = i * GROUPS + g
                pe.wait_ge(prob_ready, n + 1)
                if g == 0:
                    pe.wait_ge(v_ready, i + 1)
                    reached(pe, attn_ready, i)
                    reached(pe, rank_read, i - 1)
                for j in range(PPG):
                    pair = g * PPG + j
                    for b in range(2):
                        r = slice(b * SEQ, (b + 1) * SEQ)
                        m = mm(ps_o[r, pair * 18:(pair + 1) * 18], probT[:, g % 2, j, r],
                               v_pair[:, p, b, pair].rearrange("p h d -> p (h d)"))
                m.then_inc(av_done, 1)

            def step(i, p, twos, on):
                if "B" in on:
                    scores(i - 1, 1 - p, 0)
                if "A" in on:
                    pe.wait_ge(xhat_ready, i + 1)
                    reached(pe, kmask_ready, i)
                    two_transposes(ps_q[:, 0:256], xhat).then_inc(xT_done, 1)
                if "B" in on:
                    scores(i - 1, 1 - p, 1)
                if "C" in on:
                    pe.wait_ge(attn_ready, i - 1)
                    reached(pe, expl_ready, i - 2)
                    two_transposes(ps_c[:, 0:256], attn).then_inc(aT_done, 1)
                if "D" in on:
                    pe.wait_ge(taken_ready, i - 2)
                    mm(ps_o[:, RANK:RANK + EXPERTS], tri[:], taken[:, 1 - p, :])
                    mm(ps_o[:, RANK + EXPERTS:RANK + 2 * EXPERTS], ones_bf[:], taken[:, 1 - p, :]).then_inc(rank_done, 1)
                if "A" in on:
                    reached(pe, v_ready, i)
                    mm(ps_kv[:, 0:256], ctxT[:, p, :], wk_sb[:])
                    for h in range(2):
                        for b in range(2):
                            m = mm(ps_kv[h * SEQ:(h + 1) * SEQ, 256 + b * P:256 + (b + 1) * P],
                                   ctxT[:, p, b * SEQ:(b + 1) * SEQ], wv_sb[:, h, :])
                    m.then_inc(kv_done, 1)
                if "B" in on:
                    turn(i - 1, 0)
                if "A" in on:
                    pe.wait_ge(xhT_ready, i + 1)
                    project(ps_q[:, 256:512], xhT, wq_sb).then_inc(q_done, 1)
                if "B" in on:
                    scores(i - 1, 1 - p, 2)
                if "C" in on:
                    pe.wait_ge(attnT_ready, i - 1)
                    reached(pe, expl_ready, i - 2)
                    project(ps_c[:, 256:512], attnT, wo_sb).then_inc(wo_done, 1)
                if "B" in on:
                    turn(i - 1, 1)
                    values(i - 1, 1 - p, 0)
                    scores(i - 1, 1 - p, 3)
                    turn(i - 1, 2)
                    values(i - 1, 1 - p, 1)
                if "A" in on:
                    pe.wait_ge(q_ready, i + 1)
                    alone(pe)
                    for src, off in ((q_rot, 0), (k_rot, 256)):
                        for gq in range(GROUPS):
                            for b in range(2):
                                r = slice(b * SEQ, (b + 1) * SEQ)
                                m = mm(ps_q[r, off + gq * SEQ:off + (gq + 1) * SEQ], src[r, gq * SEQ:(gq + 1) * SEQ],
                                       const[r, C_ID + b * SEQ:C_ID + (b + 1) * SEQ])
                    m.then_inc(qkT_done, 1)
                if "C" in on:
                    pe.wait_ge(xh2_ready, i - 1)
                    two_transposes(ps_c[:, 0:256], xh2).then_inc(x2T_done, 1)
                if "B" in on:
                    turn(i - 1, 3)
                    values(i - 1, 1 - p, 2)
                if "C" in on:
                    pe.wait_ge(xh2T_ready, i - 1)
                    project(ps_c[:, 256:256 + EXPERTS], xh2T, gate_sb).then_inc(router_done, 1)
                if "B" in on:
                    values(i - 1, 1 - p, 3)

            pe.wait_ge(consts_in, 16 * 8)
            pe.wait_ge(consts_ready, 7)
            pe.wait_ge(dve_const, 7)
            pipeline(pe, step)

            pe.wait_ge(gu_in, 16 * 8)
            pe.wait_ge(slot_ready, TILES)

            def turn_block(b, u, rnd):
                p = u % 2
                if u % BG == 0:
                    pe.wait_ge(xb_in[u // BG], (rnd + 1) * 16)
                reached(pe, xbT_ready, b - 1)
                two_transposes(pp_xT[p], xb[:, u // BG, u % BG]).then_inc(xbT_done, 1)

            def gate_up_block(b, u, rnd):
                p = u % 2
                e = pe.value_load(xb[0:1, u // BG, u % BG, COL_EXP:COL_EXP + 1].bitcast(I32), min_val=0, max_val=EXPERTS - 1)
                pe.wait_ge(xbT_ready, b + 1)
                reached(pe, hid_ready, b - 1)
                for c in range(2):
                    m = mm(pp_gu[p][:, 0:2 * INNER], xbT[:, p, c, :],
                           gu_sb[:, bass.ds(e, 1), c, :].rearrange("p e n -> p (e n)"), start=c == 0, stop=c == 1)
                m.then_inc(gu_done, 1)

            def turn_hidden(b, u, rnd):
                p = u % 2
                pe.wait_ge(hid_ready, b + 1)
                reached(pe, hidT_ready, b - 1)
                t.transpose(pp_hT[p][0:INNER, 0:P], hid[:, p, :], ident).then_inc(hT_done, 1)

            def down_block(b, u, rnd):
                j, p = u % NB, u % 2
                pe.wait_ge(hidT_ready, b + 1)
                pe.wait_ge(w2_in[j], (rnd * (ROUND // NB) + u // NB + 1) * 16)
                reached(pe, yb_ready, b - 1)
                mm(pp_y[p][:, 0:DIM], hidT[:, p, :], w2_sb[:, j, :]).then_inc(y_done, 1)

            beats2(pe, {0: turn_block, 1: gate_up_block, 2: turn_hidden, 3: down_block})



def beats2(eng, stages):
    U = ROUND

    def beat(rounds, u):
        for s in sorted(stages):
            if isinstance(rounds, int) and not 0 <= rounds * U + u - s < BLOCKS:
                continue
            stages[s](rounds * U + (u - s), (u - s) % U, rounds + (u - s) // U)

    for u in range(U):
        beat(0, u)
    with eng.Fori(1, BLOCKS // U) as rounds:
        for u in range(U):
            beat(rounds, u)
    for u in range(max(stages)):
        beat(BLOCKS // U, u)


CHAIN_FULL = 30


def kernel(x, ctx_1024, fside_BxSx2_0, L0_xattn_Wq, L0_xattn_Wkv, L0_xattn_Wout, L0_xattn_bout,
           L0_ffn_gate_weight, L0_ffn_gate_up_proj, L0_ffn_down_proj):
    import concourse.bacc as bacc
    from concourse.bass_utils import run_bass_kernel_spmd

    def lay(a):
        return np.ascontiguousarray(a)

    def chunks(w):
        return lay(np.asarray(w).reshape(2, P, -1).transpose(1, 0, 2))

    wkv = np.asarray(L0_xattn_Wkv)
    const = np.zeros((P, C_END), np.float32)
    const[:, C_ID:C_ID + P] = np.eye(P)
    const[:, C_HM:C_HM + HG] = (np.arange(P)[:, None] % SEQ) // HD == np.arange(HG)
    const[:, C_IOTA:C_IOTA + EXPERTS] = np.arange(EXPERTS)
    const[:, C_DEST:C_DEST + TOPK] = np.arange(P)[:, None] * KSLOTS + np.arange(TOPK)
    const[:, C_TRI:C_TRI + P] = np.arange(P)[:, None] < np.arange(P)
    blank = np.zeros((P, ROW), np.int32)
    blank[:, COL_DEST] = 1 << 20
    arrays = {
        "x": lay(np.asarray(x).reshape(TOKENS, DIM)),
        "ctxT": lay(np.asarray(ctx_1024).reshape(TOKENS, CTX).T),
        "pos": lay(np.asarray(fside_BxSx2_0).reshape(TOKENS, 2)),
        "wq": chunks(L0_xattn_Wq),
        "wk": lay(wkv[:, :DIM]),
        "wv": lay(wkv[:, DIM:].reshape(CTX, PAIRS, 2, HD).transpose(0, 2, 1, 3).reshape(CTX, 2, DIM // 2)),
        "wo": chunks(L0_xattn_Wout),
        "bout": lay(np.broadcast_to(np.asarray(L0_xattn_bout), (P, DIM))),
        "gate": chunks(np.asarray(L0_ffn_gate_weight).T),
        "gu": lay(np.asarray(L0_ffn_gate_up_proj).transpose(2, 0, 1).reshape(2, P, EXPERTS, 2 * INNER).transpose(1, 2, 0, 3)),
        "w2": lay(np.asarray(L0_ffn_down_proj).transpose(0, 2, 1)),
        "const": const,
        "blank": blank.view(np.float32),
    }
    nc = bacc.Bacc("TRN2", target_bir_lowering=False, num_devices=1)
    aps = [nc.dram_tensor(f"in_{n}", a.shape, mybir.dt.from_np(a.dtype), kind="ExternalInput").ap() for n, a in arrays.items()]
    out = nc.dram_tensor("out", [TOKENS, DIM], F32, kind="ExternalOutput").ap()
    build(nc, *aps, out)
    r = run_bass_kernel_spmd(nc, [{f"in_{n}": a for n, a in arrays.items()}], core_ids=[0])
    return r.results[0]["out"].reshape(BATCH, SEQ, DIM)
```

```python
import math

import numpy as np

import concourse.bass as bass
from concourse import mybir
from contextlib import ExitStack

F32 = mybir.dt.float32
BF16 = mybir.dt.bfloat16
I32 = mybir.dt.int32
U32 = mybir.dt.uint32
ALU = mybir.AluOpType
ACT = mybir.ActivationFunctionType
AX = mybir.AxisListType

P = 128
BATCH, SEQ, DIM, CTX = 32, 64, 256, 128
HEADS, HD = 32, 8
EXPERTS, INNER, TOPK = 64, 96, 4
TOKENS = BATCH * SEQ
TILES = TOKENS // P
GROUPS = 4
HG = HEADS // GROUPS
PAIRS = HEADS // 2
PPG = PAIRS // GROUPS
EPS = 1e-5
SCALE = 1.0 / math.sqrt(HD)
TWO_PI = 2.0 * math.pi

ROW = DIM + 4
COL_DEST, COL_W, COL_EXP = DIM, DIM + 1, DIM + 2
BLOCKS = TOKENS * TOPK // P + EXPERTS
BG = 2
NG = 8
ROUND = BG * NG
NB = 8

C_ID, C_HM, C_IOTA, C_DEST, C_TRI, C_END = 0, 128, 136, 200, 204, 332


class Chain:

    def __init__(self, eng, sem, base=0):
        self.eng, self.sem, self.base, self.n = eng, sem, base, 0

    def after(self, instruction):
        self.n += 1
        instruction.then_inc(self.sem, 1)

    def sync(self):
        self.eng.wait_ge(self.sem, self.base + self.n)


def reached(eng, sem, value):
    if not isinstance(value, int) or value > 0:
        eng.wait_ge(sem, value)


def build(nc, x_d, ctxT_d, pos_d, wq_d, wk_d, wv_d, wo_d, bout_d, gate_d, gu_d, w2_d, const_d, blank_d, out_d):
    rows_d = nc.dram_tensor("rows_d", [BLOCKS * P, ROW], F32, kind="Internal").ap()
    res_d = nc.dram_tensor("res_d", [TOKENS * TOPK, DIM], F32, kind="Internal").ap()
    res_tok = res_d.rearrange("(t k) d -> t k d", k=TOPK)

    ctx = ExitStack()
    with ctx:
        def sb(name, shape, dt=F32):
            return ctx.enter_context(nc.sbuf_tensor(name, shape, dt))

        def sem(name):
            return ctx.enter_context(nc.semaphore(name))

        gu_sb = sb("gu_sb", [P, EXPERTS, 2, 2 * INNER])
        wq_sb = sb("wq_sb", [P, 2, DIM])
        wk_sb = sb("wk_sb", [P, DIM])
        wv_sb = sb("wv_sb", [P, 2, DIM // 2])
        wo_sb = sb("wo_sb", [P, 2, DIM])
        gate_sb = sb("gate_sb", [P, 2, EXPERTS])
        bout_sb = sb("bout_sb", [P, DIM])
        const = sb("const", [P, C_END])
        blank = sb("blank", [P, ROW])
        ident = const[:, C_ID:C_ID + P]
        hmask = const[:, C_HM:C_HM + HG]
        iota_e = const[:, C_IOTA:C_IOTA + EXPERTS]
        tri = sb("tri", [P, P], BF16)
        ones_bf = sb("ones_bf", [P, P], BF16)
        ones_e = sb("ones_e", [P, EXPERTS])
        neg_half = sb("neg_half", [P, 1])

        pos_sb = sb("pos_sb", [P, TILES, 2])
        ang = sb("ang", [P, 2, TILES, 4])
        turns = sb("turns", [P, 2, TILES, 4])
        trig = sb("trig", [P, 2, TILES, 4])
        nsin = sb("nsin", [P, TILES, 4])

        x_all = sb("x_all", [P, TILES, DIM])

        shared = sb("shared", [P, 8320])
        used = [0, 0]

        def part(phase, *dims):
            n = int(np.prod(dims))
            view = shared[:, used[phase - 1]:used[phase - 1] + n]
            used[phase - 1] += n
            names = "abcdef"[:len(dims)]
            return view.rearrange(f"p ({' '.join(names)}) -> p {' '.join(names)}", **dict(zip(names, dims)))

        ctxT = sb("ctxT", [P, 2, P])
        st1 = sb("st1", [P, 6])
        mv1 = sb("mv1", [P, 2])
        ve1 = sb("ve1", [P, 1])
        rstd1 = sb("rstd1", [P, 1])
        shift1 = sb("shift1", [P, 1])
        xhat = sb("xhat", [P, DIM])
        xhT = sb("xhT", [P, 2, P])
        k_sb = sb("k_sb", [P, DIM])
        k_cos = sb("k_cos", [P, DIM])
        k_sin = sb("k_sin", [P, DIM])
        k_rot = sb("k_rot", [P, DIM])
        q_sb = sb("q_sb", [P, DIM])
        q_cos = sb("q_cos", [P, DIM])
        q_sin = sb("q_sin", [P, DIM])
        q_rot = sb("q_rot", [P, DIM])
        q_diag = part(1, 2, GROUPS, P)
        k_mask = part(1, 2, GROUPS, HG, SEQ)
        v_pair = part(1, 2, 2, PAIRS, 2, HD + 1)

        mx = sb("mx", [P, 2, HG])
        shifted = part(1, 2, HG * SEQ)
        probT = part(1, 2, PPG, P)

        rsum = sb("rsum", [P, HEADS])
        attn = sb("attn", [P, DIM])
        attnT = sb("attnT", [P, 2, P])

        st2 = sb("st2", [P, 6])
        mv2 = sb("mv2", [P, 2])
        ve2 = sb("ve2", [P, 1])
        rstd2 = sb("rstd2", [P, 1])
        shift2 = sb("shift2", [P, 1])
        xh2 = sb("xh2", [P, 2, DIM])
        xh2T = sb("xh2T", [P, 2, P])
        nmx = sb("nmx", [P, 1])
        expl = sb("expl", [P, EXPERTS])
        esum = sb("esum", [P, 1])
        resum = sb("resum", [P, 1])
        probs = sb("probs", [P, EXPERTS])
        top8 = sb("top8", [P, 8])
        idx8 = sb("idx8", [P, 8], U32)
        idxf = sb("idxf", [P, TOPK])
        wsum = sb("wsum", [P, 1])
        wclip = sb("wclip", [P, 1])
        rwsum = sb("rwsum", [P, 1])
        chosen = sb("chosen", [P, TOPK, EXPERTS])
        taken = sb("taken", [P, EXPERTS], BF16)
        rows = sb("rows", [P, 2, TOPK, ROW])

        count = sb("count", [P, EXPERTS])
        room = sb("room", [P, EXPERTS])
        base = sb("base", [P, EXPERTS])
        base_room = sb("base_room", [P, EXPERTS])
        last = sb("last", [P, 1])
        rank = sb("rank", [P, EXPERTS])
        opens = sb("opens", [P, EXPERTS])
        newest = sb("newest", [P, EXPERTS])
        step_b = sb("step_b", [P, EXPERTS])
        spill = sb("spill", [P, EXPERTS])
        spill_b = sb("spill_b", [P, EXPERTS])
        open_b = sb("open_b", [P, EXPERTS])
        slot_e = sb("slot_e", [P, EXPERTS])
        slot_r = sb("slot_r", [P, EXPERTS])
        slot_ke = sb("slot_ke", [P, TOPK, EXPERTS])
        slot_k = sb("slot_k", [P, TOPK])
        slot_i = sb("slot_i", [P, 2, TOPK], I32)
        dest = sb("dest", [P, TOPK])

        xb = part(2, NG, BG, ROW)
        yb = part(2, NB, DIM)
        w2_sb = part(2, NB, DIM)[0:INNER]
        xbT = sb("xbT", [P, 2, 2, P])
        silu = sb("silu", [P, 2, INNER])
        hid = sb("hid", [P, 2, INNER])
        hidT = sb("hidT", [INNER, 2, P])

        NRES = 4
        gu_flat = gu_sb[:].rearrange("p e c n -> p (e c n)")
        res_cols = NRES * TOPK * DIM
        res = gu_flat[:, 0:res_cols].rearrange("p (j k d) -> p j k d", j=NRES, k=TOPK)
        fin = gu_flat[:, res_cols:res_cols + NRES * DIM].rearrange("p (j d) -> p j d", j=NRES)

        bank = [ctx.enter_context(nc.psum_tensor(f"bank{i}", [P, 512], F32)) for i in range(8)]
        ps_q, ps_kv, ps_o, ps_c = bank[0], bank[1], bank[6], bank[7]
        ps_s, ps_t = bank[2:4], bank[4:6]
        o_view = ps_o[:, 0:PAIRS * 2 * (HD + 1)].rearrange("p (h d) -> p h d", d=HD + 1)
        RANK = 256 + EXPERTS
        pp_xT, pp_gu, pp_hT, pp_y = bank[0:2], bank[2:4], bank[4:6], bank[6:8]

        const_in = sem("const_in"); weights_in = sem("weights_in"); later_in = sem("later_in"); pos_in = sem("pos_in")
        first_in = sem("first_in"); second_in = sem("second_in"); rest_in = sem("rest_in")
        ctx_in = [sem(f"ctx_in{p}") for p in range(2)]
        consts_ready = sem("consts_ready"); dve_const = sem("dve_const")
        angles_ready = sem("angles_ready"); trig_ready = sem("trig_ready")
        blank_rows = sem("blank_rows")
        gu_in = sem("gu_in")
        var1_ready = sem("var1_ready"); rstd1_ready = sem("rstd1_ready"); shift1_ready = sem("shift1_ready"); xhat_ready = sem("xhat_ready")
        xT_done = sem("xT_done"); xhT_ready = sem("xhT_ready")
        kv_done = sem("kv_done"); q_done = sem("q_done")
        k_in = sem("k_in"); q_in = sem("q_in"); kparts_ready = sem("kparts_ready"); qparts_ready = sem("qparts_ready")
        k_ready = sem("k_ready"); q_ready = sem("q_ready")
        kT_done = sem("kT_done"); qT_done = sem("qT_done")
        qdiag_ready = sem("qdiag_ready"); kmask_ready = sem("kmask_ready"); v_ready = sem("v_ready")
        s_done = sem("s_done"); max_ready = sem("max_ready"); shifted_ready = sem("shifted_ready")
        t_done = sem("t_done"); prob_ready = sem("prob_ready"); av_done = sem("av_done")
        rsum_ready = sem("rsum_ready"); attn_ready = sem("attn_ready")
        aT_done = sem("aT_done"); attnT_ready = sem("attnT_ready"); wo_done = sem("wo_done")
        bias_added = sem("bias_added"); x2_ready = sem("x2_ready")
        var2_ready = sem("var2_ready"); rstd2_ready = sem("rstd2_ready"); shift2_ready = sem("shift2_ready"); xh2_ready = sem("xh2_ready")
        slot_e_ready = sem("slot_e_ready"); step_ready = sem("step_ready"); open_ready = sem("open_ready")
        base_moved = sem("base_moved"); base_ready = sem("base_ready")
        x2T_done = sem("x2T_done"); xh2T_ready = sem("xh2T_ready"); router_done = sem("router_done")
        nmx_ready = sem("nmx_ready"); expl_ready = sem("expl_ready")
        taken_ready = sem("taken_ready"); rank_done = sem("rank_done"); rank_read = sem("rank_read"); slot_ready = sem("slot_ready")
        rowvals_ready = sem("rowvals_ready")
        scattered = [sem(f"scattered{p}") for p in range(2)]
        dve_step = sem("dve_step")
        passed = sem("passed")
        xb_in = [sem(f"xb_in{n}") for n in range(NG)]
        w2_in = [sem(f"w2_in{n}") for n in range(NB)]
        xbT_done = sem("xbT_done"); xbT_ready = sem("xbT_ready"); gu_done = sem("gu_done")
        silu_ready = sem("silu_ready"); hid_ready = sem("hid_ready"); hT_done = sem("hT_done")
        hidT_ready = sem("hidT_ready"); y_done = sem("y_done"); yb_ready = sem("yb_ready")
        y_scattered = [sem(f"y_scattered{n}") for n in range(NB)]
        res_in = [sem(f"res_in{j}") for j in range(NRES)]
        sum_ready = sem("sum_ready"); fin_ready = sem("fin_ready")
        fin_out = [sem(f"fin_out{j}") for j in range(NRES)]

        def factors(i):
            cos = trig[:, 1, bass.ds(i, 1), :].unsqueeze(3).to_broadcast([P, HEADS, 4, 2])
            return (cos, nsin[:, bass.ds(i, 1), :].to_broadcast([P, HEADS, 4]),
                    trig[:, 0, bass.ds(i, 1), :].to_broadcast([P, HEADS, 4]))

        def alone(eng):
            eng.sem_inc(passed, 1)

        INIT = BLOCKS // 8
        GU_STEP = EXPERTS // 8

        def pipeline(eng, step, total=None, full=0):
            def stages(i):
                on = {"L"} if i + 1 < TILES else set()
                return on | {name for lag, name in enumerate("ABVMRE") if 0 <= i - lag < TILES}

            def run(i, p, half, on, base):
                if total is None:
                    return step(i, p, half, on)
                return step(i, p, half, on, base)

            everything = set("LABVMRE")
            for i in range(5):
                n = run(i, i % 2, i // 2, stages(i), total)
                total = total + n if total is not None else None
            start = total
            with eng.Fori(2, TILES // 2 - 1) as twos:
                base = None if start is None else twos * (2 * full) + (start - 4 * full)
                n = run(twos * 2 + 1, 1, twos, everything, base)
                m = run(twos * 2 + 2, 0, twos + 1, everything, None if start is None else base + full)
                assert start is None or (n == full and m == full), (n, m)
            total = None if start is None else start + full * (TILES - 6)
            for i in range(TILES - 1, TILES + 5):
                n = run(i, i % 2, i // 2, stages(i), total)
                total = total + n if total is not None else None

        block = ctx.enter_context(nc.Block())

        @block.sync
        def _(sp):
            tiles = x_d.rearrange("(t p) d -> p t d", p=P)
            sp.dma_start(x_all[:, 0:1], tiles[:, 0:1]).then_inc(first_in, 16)
            sp.dma_start(pos_sb[:], pos_d.rearrange("(t p) a -> p t a", p=P)).then_inc(pos_in, 16)
            sp.dma_start(const[:], const_d).then_inc(const_in, 16)
            sp.dma_start(ctxT[:, 0], ctxT_d[:, 0:P]).then_inc(ctx_in[0], 16)
            sp.dma_start(wk_sb[:], wk_d).then_inc(weights_in, 16)
            sp.dma_start(wv_sb[:], wv_d).then_inc(weights_in, 16)
            sp.dma_start(wq_sb[:], wq_d).then_inc(weights_in, 16)
            sp.dma_start(x_all[:, 1:2], tiles[:, 1:2]).then_inc(second_in, 16)
            sp.dma_start(bout_sb[:], bout_d).then_inc(later_in, 16)
            sp.dma_start(wo_sb[:], wo_d).then_inc(later_in, 16)
            sp.dma_start(gate_sb[:], gate_d).then_inc(later_in, 16)
            sp.dma_start(blank[:], blank_d).then_inc(later_in, 16)
            sp.dma_start(x_all[:, 2:TILES], tiles[:, 2:TILES]).then_inc(rest_in, 16)
            sp.wait_ge(later_in, 16 * 4)
            view = rows_d.rearrange("(b p) c -> p b c", p=P)
            for k in range(8):
                reached(sp, kv_done, k // 2 + 1)
                sp.dma_start(view[:, k * INIT:(k + 1) * INIT, :],
                             blank[:].unsqueeze(1).to_broadcast([P, INIT, ROW])).then_inc(blank_rows, 16)
            for k in range(8):
                sp.wait_ge(kv_done, k + 5)
                r = slice(k * GU_STEP, (k + 1) * GU_STEP)
                sp.dma_start(gu_sb[:, r], gu_d[:, r]).then_inc(gu_in, 16)

            for p in range(2):
                sp.wait_ge(scattered[p], 16 * TOPK * TILES // 2)

            loads = rows_d.rearrange("(g j p) c -> g p j c", p=P, j=BG)

            def load_rows(rnd, n):
                if not isinstance(rnd, int) or rnd > 0:
                    for j in range(BG):
                        u = n * BG + j
                        sp.wait_ge(y_scattered[u % NB], ((rnd - 1) * (ROUND // NB) + u // NB + 1) * 16)
                sp.dma_start(xb[:, n], loads[bass.ds(rnd * NG + n, 1)].rearrange("g p j c -> (g p) j c")).then_inc(xb_in[n], 16)

            def load_down(rnd, n):
                sp.wait_ge(xb_in[n], (rnd + 1) * 16)
                alone(sp)
                for j in range(BG):
                    u = n * BG + j
                    e = sp.value_load(xb[0:1, n, j, COL_EXP:COL_EXP + 1].bitcast(I32), min_val=0, max_val=EXPERTS - 1)
                    reached(sp, y_done, rnd * ROUND + (u - NB + 1))
                    sp.dma_start(w2_sb[:, u % NB, :], w2_d[bass.ds(e, 1)].rearrange("e i d -> (e i) d")).then_inc(w2_in[u % NB], 16)

            AHEAD = 2
            for n in range(AHEAD):
                load_rows(0, n)
            for n in range(NG - AHEAD):
                load_rows(0, n + AHEAD)
                load_down(0, n)
            with sp.Fori(1, BLOCKS // ROUND) as rnd:
                for n in range(NG):
                    load_rows(rnd, n)
                    if n < AHEAD:
                        load_down(rnd - 1, n + NG - AHEAD)
                    else:
                        load_down(rnd, n - AHEAD)
            for n in range(NG - AHEAD, NG):
                load_down(BLOCKS // ROUND - 1, n)

            for n in range(NB):
                sp.wait_ge(y_scattered[n], BLOCKS // NB * 16)

            def load_results(i, j):
                reached(sp, fin_ready, i - NRES + 1)
                sp.dma_start(res[:, j], res_tok[bass.ds(i * P, P)]).then_inc(res_in[j], 16)

            for j in range(NRES):
                load_results(j, j)
            with sp.Fori(1, TILES // NRES) as fours:
                i = fours * NRES
                for j in range(NRES):
                    load_results(i + j, j)

        @block.gpsimd
        def _(pool):
            g = nc.gpsimd
            g.memset(neg_half[:], -0.5).then_inc(consts_ready, 1)
            g.memset(ones_e[:], 1.0).then_inc(consts_ready, 1)
            g.memset(ones_bf[:], 1.0).then_inc(consts_ready, 1)
            g.memset(q_diag[:], 0.0).then_inc(consts_ready, 1)
            g.memset(v_pair[:], 0.0).then_inc(consts_ready, 1)
            pool.wait_ge(consts_ready, 5)
            for h in range(2):
                r = slice(h * SEQ, (h + 1) * SEQ)
                g.memset(v_pair[r, :, :, :, h, HD:HD + 1].rearrange("p s b n o -> p (s b n) o"), 1.0).then_inc(consts_ready, 1)

            def rstd(var, out, ready, n, done):
                pool.wait_ge(ready, n)
                g.tensor_tensor(out[:], var[:], neg_half[:], ALU.pow).then_inc(done, 1)

            def rotate(i, src, cos_part, sin_part, out, parts_ready, ready):
                alone(pool)
                cos, sin_e, sin_o = factors(i)
                s, c, o = (x[:].rearrange("p (h c two) -> p h c two", c=4, two=2) for x in (src, cos_part, sin_part))
                g.tensor_tensor(c, s, cos, ALU.mult)
                g.tensor_tensor(o[:, :, :, 0], s[:, :, :, 1], sin_e, ALU.mult)
                g.tensor_tensor(o[:, :, :, 1], s[:, :, :, 0], sin_o, ALU.mult).then_inc(parts_ready, 1)
                pool.wait_ge(parts_ready, i + 1)
                g.tensor_tensor(out[:], cos_part[:], sin_part[:], ALU.add).then_inc(ready, 1)

            def dispatch(q, ks):
                for k in ks:
                    g.indirect_dma_start(rows_d, bass.IndirectOffsetOnAxis(ap=slot_i[:, q, k:k + 1], axis=0),
                                         rows[:, q, k, :], None).then_inc(scattered[q], 16)

            def step(i, p, half, on):
                if "E" in on:
                    pool.wait_ge(rowvals_ready, i - 4)
                    alone(pool)
                    pool.wait_ge(slot_ready, i - 4)
                    alone(pool)
                    if "B" in on:
                        dispatch(1 - p, range(2))
                if "M" in on:
                    reached(pool, xh2_ready, i - 3)
                    rstd(ve2, rstd2, var2_ready, i - 2, rstd2_ready)
                if "L" in on:
                    reached(pool, xhat_ready, i + 1)
                    rstd(ve1, rstd1, var1_ready, i + 2, rstd1_ready)
                if "A" in on:
                    pool.wait_ge(k_in, i + 1)
                    reached(pool, kT_done, i)
                    rotate(i, k_sb, k_cos, k_sin, k_rot, kparts_ready, k_ready)
                    pool.wait_ge(q_in, i + 1)
                    reached(pool, qT_done, i)
                    rotate(i, q_sb, q_cos, q_sin, q_rot, qparts_ready, q_ready)
                if "E" in on:
                    dispatch(1 - p, range(2 if "B" in on else 0, TOPK))
                if "A" in on:
                    if isinstance(i, int) and i == 0:
                        pool.wait_ge(later_in, 16 * 4)
                    pool.wait_ge(xhat_ready, i + 1)
                    tile = x_all[:, bass.ds(i, 1), :].rearrange("p o d -> p (o d)")
                    g.tensor_tensor(tile, tile, bout_sb[:], ALU.add).then_inc(bias_added, 1)
                if "R" in on:
                    pool.wait_ge(rank_read, i - 3)
                    g.tensor_tensor(slot_e[:], rank[:], base[:], ALU.add).then_inc(slot_e_ready, 1)
                    pool.wait_ge(step_ready, i - 3)
                    g.tensor_tensor(open_b[:], step_b[:], opens[:], ALU.mult).then_inc(open_ready, 1)
                    pool.wait_ge(open_ready, i - 3)
                    pool.wait_ge(slot_e_ready, i - 3)
                    g.tensor_tensor(base[:], base[:], open_b[:], ALU.add).then_inc(base_moved, 1)
                    pool.wait_ge(base_moved, i - 3)
                    g.tensor_tensor(base_room[:], base[:], room[:], ALU.add).then_inc(base_ready, 1)
                if isinstance(i, int) and i == 4:
                    pool.wait_ge(blank_rows, 16 * 8)

            pool.wait_ge(consts_ready, 7)
            rstd(ve1, rstd1, var1_ready, 1, rstd1_ready)
            pool.wait_ge(dve_const, 7)
            pipeline(pool, step)

            with pool.Fori(0, BLOCKS // ROUND) as rnd:
                for u in range(ROUND):
                    pool.wait_ge(yb_ready, rnd * ROUND + (u + 1))
                    alone(pool)
                    g.indirect_dma_start(
                        res_d, bass.IndirectOffsetOnAxis(ap=xb[:, u // BG, u % BG, COL_DEST:COL_DEST + 1].bitcast(I32), axis=0),
                        yb[:, u % NB, :], None, bounds_check=TOKENS * TOPK - 1, oob_is_err=False).then_inc(y_scattered[u % NB], 16)

        @block.scalar
        def _(act):
            a = nc.scalar

            def kmask_part(i, p, hs):
                for h in hs:
                    m = a.activation(k_mask[:, p, :, h, :], ps_kv[:, 0:256].rearrange("p (g k) -> p g k", g=GROUPS),
                                     ACT.Copy, scale=hmask[:, h:h + 1])
                return m

            def exp_group(i, g):
                n = i * GROUPS + g
                act.wait_ge(t_done, n + 1)
                reached(act, av_done, n - 1)
                a.activation(probT[:, g % 2].rearrange("p j q -> p (j q)"), ps_t[g % 2][:], ACT.Exp,
                             scale=SCALE).then_inc(prob_ready, 1)

            def turned_x(i):
                act.wait_ge(xT_done, i + 1)
                reached(act, q_done, i)
                a.copy(xhT[:].rearrange("p c t -> p (c t)"), ps_q[:, 0:256]).then_inc(xhT_ready, 1)

            def normed(out, x, rstd_, shift_):
                return a.activation(out, x, ACT.Identity, scale=rstd_[:, 0:1], bias=shift_[:, 0:1])

            def x_tile(i):
                return x_all[:, bass.ds(i, 1), :].rearrange("p o d -> p (o d)")

            def step(i, p, half, on):
                q = 1 - p
                if "L" in on:
                    reached(act, kv_done, i)
                    act.dma_start(ctxT[:, q, :], ctxT_d[:, bass.ds((i + 1) * P, P)]).then_inc(ctx_in[q], 16)
                if "V" in on:
                    exp_group(i - 2, 3)
                if "R" in on:
                    if not isinstance(i, int) or i >= 6:
                        act.wait_ge(scattered[p], 16 * TOPK * (half + -2))
                    act.wait_ge(xh2_ready, i - 3)
                    for k in range(2):
                        a.copy(rows[:, p, k, 0:DIM], xh2[:, p, :])
                if "A" in on:
                    act.wait_ge(kv_done, i + 1)
                    reached(act, kparts_ready, i)
                    a.copy(k_sb[:], ps_kv[:, 0:256]).then_inc(k_in, 1)
                if "R" in on:
                    for k in range(2, TOPK):
                        m = a.copy(rows[:, p, k, 0:DIM], xh2[:, p, :])
                    m.then_inc(rowvals_ready, 1)
                if "M" in on:
                    act.wait_ge(shift2_ready, i - 2)
                    reached(act, rowvals_ready, i - 4)
                    reached(act, x2T_done, i - 4)
                    normed(xh2[:, q, :], x_tile(i + -3), rstd2, shift2).then_inc(xh2_ready, 1)
                if "A" in on:
                    act.wait_ge(q_done, i + 1)
                    reached(act, qparts_ready, i)
                    a.copy(q_sb[:], ps_q[:, 256:512]).then_inc(q_in, 1)
                if "L" in on:
                    act.wait_ge(shift1_ready, i + 2)
                    reached(act, xT_done, i + 1)
                    normed(xhat[:], x_tile(i + 1), rstd1, shift1).then_inc(xhat_ready, 1)
                if "B" in on:
                    exp_group(i - 1, 0)
                if "M" in on:
                    act.wait_ge(x2T_done, i - 2)
                    reached(act, router_done, i - 3)
                    a.copy(xh2T[:].rearrange("p c t -> p (c t)"), ps_c[:, 0:256]).then_inc(xh2T_ready, 1)
                if "A" in on:
                    if not isinstance(i, int) or i >= 2:
                        act.wait_ge(av_done, GROUPS * (i - 1))
                    for h in range(2):
                        r = slice(h * SEQ, (h + 1) * SEQ)
                        m = a.copy(v_pair[r, p, :, :, h, 0:HD],
                                   ps_kv[r, 256:512].rearrange("p (b n d) -> p b n d", b=2, d=HD))
                    m.then_inc(v_ready, 1)
                if "B" in on:
                    exp_group(i - 1, 1)
                if "A" in on:
                    act.wait_ge(kT_done, i + 1)
                    if not isinstance(i, int) or i >= 2:
                        act.wait_ge(s_done, GROUPS * (i - 1))
                    kmask_part(i, p, range(0, 3))
                if "M" in on:
                    reached(act, taken_ready, i - 3)
                    act.wait_ge(nmx_ready, i - 2)
                    a.activation(expl[:], ps_c[:, 256:256 + EXPERTS], ACT.Exp, bias=nmx[:, 0:1],
                                 accum_out=esum[:, 0:1]).then_inc(expl_ready, 1)
                if "A" in on:
                    kmask_part(i, p, range(3, 4))
                if "V" in on:
                    act.wait_ge(aT_done, i - 1)
                    reached(act, wo_done, i - 2)
                    a.copy(attnT[:].rearrange("p c t -> p (c t)"), ps_c[:, 0:256]).then_inc(attnT_ready, 1)
                if "A" in on:
                    kmask_part(i, p, range(4, 5))
                    act.wait_ge(qT_done, i + 1)
                    for b in range(2):
                        r = slice(b * SEQ, (b + 1) * SEQ)
                        m = a.copy(q_diag[r, p, :, r], ps_q[r, 0:256].rearrange("p (g q) -> p g q", g=GROUPS))
                    m.then_inc(qdiag_ready, 1)
                if "B" in on:
                    exp_group(i - 1, 2)
                if "A" in on:
                    kmask_part(i, p, range(5, HG)).then_inc(kmask_ready, 1)
                if "L" in on:
                    turned_x(i + 1)

            act.wait_ge(shift1_ready, 1)
            normed(xhat[:], x_tile(0), rstd1, shift1).then_inc(xhat_ready, 1)
            act.wait_ge(angles_ready, 1)
            a.activation(trig[:], ang[:], ACT.Sin).then_inc(trig_ready, 1)
            act.wait_ge(const_in, 16)
            act.wait_ge(consts_ready, 7)
            a.activation(expl[:, 0:1], neg_half[:], ACT.Exp).then_inc(passed, 1)
            turned_x(0)
            pipeline(act, step)

            def silu_block(b, u, rnd):
                p = u % 2
                act.wait_ge(gu_done, b + 1)
                reached(act, hid_ready, b - 1)
                a.activation(silu[:, p, :], pp_gu[p][:, 0:INNER], ACT.Silu).then_inc(silu_ready, 1)

            def hidT_block(b, u, rnd):
                p = u % 2
                act.wait_ge(hT_done, b + 1)
                reached(act, y_done, b - 1)
                a.copy(hidT[:, p, :], pp_hT[p][0:INNER, 0:P]).then_inc(hidT_ready, 1)

            def weigh_block(b, u, rnd):
                act.wait_ge(y_done, b + 1)
                reached(act, y_scattered[u % NB], (rnd * (ROUND // NB) + u // NB) * 16)
                a.activation(yb[:, u % NB, :], pp_y[u % 2][:, 0:DIM], ACT.Copy,
                             scale=xb[:, u // BG, u % BG, COL_W:COL_W + 1]).then_inc(yb_ready, 1)

            beats2(act, {1: silu_block, 2: hidT_block,
                         3: weigh_block})

            def store(i, j):
                act.wait_ge(fin_ready, i + 1)
                act.dma_start(out_d[bass.ds(i * P, P), :], fin[:, j, :]).then_inc(fin_out[j], 16)

            for j in range(NRES):
                store(j, j)
            with act.Fori(1, TILES // NRES) as fours:
                i = fours * NRES
                for j in range(NRES):
                    store(i + j, j)
            for j in range(NRES):
                act.wait_ge(fin_out[j], 16 * TILES // NRES)

        @block.vector
        def _(dve):
            v = nc.vector
            first = Chain(dve, dve_step)
            dve.wait_ge(first_in, 16)
            first.after(v.bn_stats(st1[:], x_all[:, 0, :]))
            first.sync()
            first.after(v.bn_aggr(mv1[:], st1[:]))
            first.sync()
            v.tensor_scalar(ve1[:], mv1[:, 1:2], EPS, None, ALU.add).then_inc(var1_ready, 1)
            prep = Chain(dve, dve_const)

            def link(instruction):
                prep.after(instruction)
                prep.sync()

            dve.wait_ge(pos_in, 16)
            for axis in range(2):
                for f in range(2):
                    m = v.tensor_scalar(ang[:, 0, :, 2 * axis + f], pos_sb[:, :, axis], 10000.0 ** (-f / 2), None, ALU.mult)
            link(m)
            dve.wait_ge(rstd1_ready, 1)
            v.scalar_tensor_tensor(shift1[:], mv1[:, 0:1], -1.0, rstd1[:], ALU.mult, ALU.mult).then_inc(shift1_ready, 1)
            link(v.tensor_scalar(ang[:, 1], ang[:, 0], math.pi / 2, None, ALU.add))
            NEAREST = 1.5 * 2.0 ** 23
            HI = 6.28125
            link(v.tensor_scalar(turns[:], ang[:], 1.0 / TWO_PI, NEAREST, ALU.mult, ALU.add))
            link(v.tensor_scalar(turns[:], turns[:], NEAREST, None, ALU.subtract))
            link(v.scalar_tensor_tensor(ang[:], turns[:], -HI, ang[:], ALU.mult, ALU.add))
            link(v.scalar_tensor_tensor(ang[:], turns[:], -(TWO_PI - HI), ang[:], ALU.mult, ALU.add))
            v.tensor_scalar(ang[:], ang[:], 3.1415925, -3.1415925, ALU.min, ALU.max).then_inc(angles_ready, 1)
            dve.wait_ge(const_in, 16)
            v.tensor_copy(tri[:], const[:, C_TRI:C_TRI + P])
            v.tensor_copy(dest[:], const[:, C_DEST:C_DEST + TOPK])
            v.memset(count[:], 0.0)
            v.memset(room[:], 0.0)
            v.memset(base[:], 0.0)
            v.memset(base_room[:], 0.0)
            v.memset(last[:], -1.0)
            v.memset(rows[:, :, :, COL_EXP + 1:ROW], 0.0)
            dve.wait_ge(trig_ready, 1)
            link(v.tensor_scalar(nsin[:], trig[:, 0], -1.0, None, ALU.mult))
            dve.wait_ge(consts_ready, 7)

            def scores_of(g):
                return ps_s[g % 2][:].rearrange("p (h k) -> p h k", h=HG)

            def group_max(i, g):
                dve.wait_ge(s_done, i * GROUPS + g + 1)
                v.tensor_reduce(mx[:, g % 2, :], scores_of(g), AX.X, ALU.max).then_inc(max_ready, 1)

            def group_shift(i, g):
                n = i * GROUPS + g
                dve.wait_ge(max_ready, n + 1)
                reached(dve, t_done, n - 1)
                v.tensor_tensor(shifted[:, g % 2, :].rearrange("p (h k) -> p h k", h=HG), scores_of(g),
                                mx[:, g % 2, :].unsqueeze(2).to_broadcast([P, HG, SEQ]),
                                ALU.subtract).then_inc(shifted_ready, 1)

            def x_tile(i):
                return x_all[:, bass.ds(i, 1), :].rearrange("p o d -> p (o d)")

            def step(i, p, half, on, base_n):
                ch = Chain(dve, dve_step, base_n)

                def link(x):
                    ch.after(x)
                    ch.sync()

                B, V, M, R, L = (x in on for x in "BVMRL")
                q = 1 - p
                if M:
                    dve.wait_ge(wo_done, i - 2)
                    dve.wait_ge(bias_added, i - 2)
                    v.tensor_tensor(x_tile(i + -3), ps_c[:, 256:512], x_tile(i + -3), ALU.add).then_inc(x2_ready, 1)
                if L:
                    if isinstance(i, int) and i < 2:
                        dve.wait_ge((second_in, rest_in)[i], 16)
                    ch.after(v.bn_stats(st1[:], x_tile(i + 1)))
                if M:
                    dve.wait_ge(x2_ready, i - 2)
                    alone(dve)
                    ch.after(v.bn_stats(st2[:], x_tile(i + -3)))
                if L or M:
                    ch.sync()
                    alone(dve)
                if L:
                    ch.after(v.bn_aggr(mv1[:], st1[:]))
                if M:
                    ch.after(v.bn_aggr(mv2[:], st2[:]))
                if B:
                    group_max(i - 1, 0)
                if M:
                    ch.sync()
                    v.tensor_scalar(ve2[:], mv2[:, 1:2], EPS, None, ALU.add).then_inc(var2_ready, 1)
                if L:
                    ch.sync()
                    v.tensor_scalar(ve1[:], mv1[:, 1:2], EPS, None, ALU.add).then_inc(var1_ready, 1)
                if R:
                    dve.wait_ge(expl_ready, i - 3)
                    ch.after(v.reciprocal(resum[:], esum[:]))
                if B:
                    group_shift(i - 1, 0)
                if R:
                    ch.sync()
                    ch.after(v.tensor_scalar(probs[:], expl[:], resum[:, 0:1], None, ALU.mult))
                if M:
                    dve.wait_ge(rstd2_ready, i - 2)
                    reached(dve, xh2_ready, i - 3)
                    v.scalar_tensor_tensor(shift2[:], mv2[:, 0:1], -1.0, rstd2[:], ALU.mult, ALU.mult).then_inc(shift2_ready, 1)
                if R:
                    ch.sync()
                    alone(dve)
                if R:
                    ch.after(v.max(top8[:], probs[:]))
                if R:
                    ch.sync()
                    alone(dve)
                    ch.after(v.max_index(idx8[:], top8[:], probs[:]))
                if L:
                    dve.wait_ge(rstd1_ready, i + 2)
                    reached(dve, xhat_ready, i + 1)
                    v.scalar_tensor_tensor(shift1[:], mv1[:, 0:1], -1.0, rstd1[:], ALU.mult, ALU.mult).then_inc(shift1_ready, 1)
                if B:
                    group_max(i - 1, 1)
                if R:
                    ch.sync()
                    ch.after(v.tensor_copy(idxf[:], idx8[:, 0:TOPK]))
                    ch.after(v.tensor_reduce(wsum[:], top8[:, 0:TOPK], AX.X, ALU.add))
                if B:
                    group_shift(i - 1, 1)
                if R:
                    ch.sync()
                    ch.after(v.tensor_tensor(chosen[:], iota_e.unsqueeze(1).to_broadcast([P, TOPK, EXPERTS]),
                                             idxf[:].unsqueeze(2).to_broadcast([P, TOPK, EXPERTS]), ALU.is_equal))
                    ch.after(v.tensor_scalar(wclip[:], wsum[:], 1e-12, None, ALU.max))
                if R:
                    ch.sync()
                    with nc.allow_low_precision(reason="zeros and ones"):
                        v.tensor_reduce(taken[:], chosen[:].rearrange("p k e -> p e k"), AX.X, ALU.add).then_inc(taken_ready, 1)
                    ch.after(v.reciprocal(rwsum[:], wclip[:]))
                if V:
                    dve.wait_ge(av_done, GROUPS * (i - 1))
                    v.reciprocal(rsum[:], o_view[:, :, HD]).then_inc(rsum_ready, 1)
                if V:
                    dve.wait_ge(rsum_ready, i - 1)
                    reached(dve, aT_done, i - 2)
                    v.tensor_tensor(attn[:].rearrange("p (h d) -> p h d", d=HD), o_view[:, :, 0:HD],
                                    rsum[:].unsqueeze(2).to_broadcast([P, HEADS, HD]), ALU.mult).then_inc(attn_ready, 1)
                if B:
                    group_max(i - 1, 2)
                if R:
                    dve.wait_ge(rank_done, i - 3)
                    v.tensor_tensor(rank[:], ps_c[:, RANK:RANK + EXPERTS], count[:], ALU.add)
                    v.tensor_tensor(count[:], ps_c[:, RANK + EXPERTS:RANK + 2 * EXPERTS], count[:], ALU.add).then_inc(rank_read, 1)
                if M:
                    dve.wait_ge(router_done, i - 2)
                    v.tensor_reduce(nmx[:], ps_c[:, 256:256 + EXPERTS], AX.X, ALU.max, negate=True).then_inc(nmx_ready, 1)
                if B:
                    group_shift(i - 1, 2)
                if R:
                    dve.wait_ge(rank_read, i - 3)
                    reached(dve, base_ready, i - 4)
                    ch.after(v.tensor_tensor(opens[:], count[:], room[:], ALU.is_gt))
                    ch.after(v.tensor_tensor(spill[:], rank[:], room[:], ALU.is_ge))
                if B:
                    group_max(i - 1, 3)
                if R:
                    ch.sync()
                    ch.after(v.tensor_tensor_scan(newest[:], ones_e[:], opens[:], last[:, 0:1], ALU.mult, ALU.add))
                    dve.wait_ge(rowvals_ready, i - 3)
                    v.tensor_scalar(rows[:, p, :, COL_W], top8[:, 0:TOPK], rwsum[:, 0:1], None, ALU.mult)
                if B:
                    group_shift(i - 1, 3)
                if R:
                    ch.sync()
                    ch.after(v.scalar_tensor_tensor(step_b[:], newest[:], float(P), base_room[:], ALU.mult, ALU.subtract))
                    v.scalar_tensor_tensor(room[:], opens[:], float(P), room[:], ALU.mult, ALU.add).then_inc(step_ready, 1)
                    v.tensor_copy(last[:], newest[:, EXPERTS - 1:EXPERTS])
                    ch.sync()
                    ch.after(v.tensor_tensor(spill_b[:], spill[:], step_b[:], ALU.mult))
                    ch.after(v.tensor_copy(rows[:, p, :, COL_DEST].bitcast(I32), dest[:]))
                    v.tensor_copy(rows[:, p, :, COL_EXP].bitcast(I32), idx8[:, 0:TOPK])
                    ch.sync()
                    dve.wait_ge(slot_e_ready, i - 3)
                    ch.after(v.tensor_tensor(slot_r[:], slot_e[:], spill_b[:], ALU.add))
                    ch.after(v.tensor_scalar(dest[:], dest[:], float(P * TOPK), None, ALU.add))
                    ch.sync()
                    link(v.tensor_tensor(slot_ke[:], chosen[:], slot_r[:].unsqueeze(1).to_broadcast([P, TOPK, EXPERTS]), ALU.mult))
                    link(v.tensor_reduce(slot_k[:], slot_ke[:], AX.X, ALU.add))
                    if not isinstance(i, int) or i >= 6:
                        dve.wait_ge(scattered[p], 16 * TOPK * (half + -2))
                    v.tensor_copy(slot_i[:, p, :], slot_k[:]).then_inc(slot_ready, 1)
                return ch.n

            pipeline(dve, step, first.n, CHAIN_FULL)

            def xbT_block(b, u, rnd):
                p = u % 2
                dve.wait_ge(xbT_done, b + 1)
                reached(dve, gu_done, b - 1)
                v.tensor_copy(xbT[:, p].rearrange("p c t -> p (c t)"), pp_xT[p][:, 0:DIM]).then_inc(xbT_ready, 1)

            def hid_block(b, u, rnd):
                p = u % 2
                dve.wait_ge(silu_ready, b + 1)
                reached(dve, hT_done, b - 1)
                v.tensor_tensor(hid[:, p, :], pp_gu[p][:, INNER:2 * INNER], silu[:, p, :], ALU.mult).then_inc(hid_ready, 1)

            beats2(dve, {0: xbT_block, 1: hid_block})

            def finish(i, j, k):
                dve.wait_ge(res_in[j], (k + 1) * 16)
                if not isinstance(i, int):
                    dve.wait_ge(fin_out[j], k * 16)
                v.tensor_reduce(fin[:, j, :], res[:, j].rearrange("p k d -> p d k"), AX.X, ALU.add).then_inc(sum_ready, 1)
                dve.wait_ge(sum_ready, i + 1)
                v.tensor_tensor(fin[:, j, :], fin[:, j, :], x_tile(i), ALU.add).then_inc(fin_ready, 1)

            for j in range(NRES):
                finish(j, j, 0)
            with dve.Fori(1, TILES // NRES) as fours:
                i = fours * NRES
                for j in range(NRES):
                    finish(i + j, j, fours)

        @block.tensor
        def _(pe):
            t = nc.tensor

            def mm(out, lhsT, rhs, start=True, stop=True):
                return t.matmul(out, lhsT, rhs, start=start, stop=stop)

            def two_transposes(ps, src):
                for c in range(2):
                    m = t.transpose(ps[:, c * P:(c + 1) * P], src[:, c * P:(c + 1) * P], ident)
                return m

            def project(ps, lhsT, w):
                for c in range(2):
                    m = mm(ps, lhsT[:, c, :], w[:, c, :], start=c == 0, stop=c == 1)
                return m

            def scores(i, p, g):
                n = i * GROUPS + g
                if g == 0:
                    pe.wait_ge(qdiag_ready, i + 1)
                    pe.wait_ge(kmask_ready, i + 1)
                reached(pe, shifted_ready, n - 1)
                mm(ps_s[g % 2][:], q_diag[:, p, g, :], k_mask[:, p, g].rearrange("p h k -> p (h k)")).then_inc(s_done, 1)

            def turn(i, g):
                n = i * GROUPS + g
                pe.wait_ge(shifted_ready, n + 1)
                reached(pe, prob_ready, n - 1)
                for j in range(PPG):
                    m = t.transpose(ps_t[g % 2][:, j * P:(j + 1) * P], shifted[:, g % 2, j * P:(j + 1) * P], ident)
                m.then_inc(t_done, 1)

            def values(i, p, g):
                n = i * GROUPS + g
                pe.wait_ge(prob_ready, n + 1)
                if g == 0:
                    pe.wait_ge(v_ready, i + 1)
                    reached(pe, attn_ready, i)
                sixteen, b = divmod(g, 2)
                for j in range(PPG):
                    for row in range(2):
                        pair = (2 * sixteen + row) * PPG + j
                        m = mm(ps_o[b * SEQ:(b + 1) * SEQ, pair * 18:(pair + 1) * 18],
                               probT[:, g % 2, j, row * SEQ:(row + 1) * SEQ],
                               v_pair[:, p, b, pair].rearrange("p h d -> p (h d)"))
                m.then_inc(av_done, 1)

            def turn_x(i):
                pe.wait_ge(xhat_ready, i + 1)
                reached(pe, qdiag_ready, i)
                two_transposes(ps_q[:, 0:256], xhat).then_inc(xT_done, 1)

            def step(i, p, half, on):
                q = 1 - p
                if "V" in on:
                    turn(i - 2, 3)
                if "B" in on:
                    scores(i - 1, q, 0)
                if "A" in on:
                    reached(pe, kmask_ready, i)
                    pe.wait_ge(ctx_in[p], 16 * (half + 1))
                    mm(ps_kv[:, 0:256], ctxT[:, p, :], wk_sb[:])
                    for h in range(2):
                        for b in range(2):
                            m = mm(ps_kv[h * SEQ:(h + 1) * SEQ, 256 + b * P:256 + (b + 1) * P],
                                   ctxT[:, p, b * SEQ:(b + 1) * SEQ], wv_sb[:, h, :])
                    m.then_inc(kv_done, 1)
                if "V" in on:
                    values(i - 2, p, 2)
                if "B" in on:
                    scores(i - 1, q, 1)
                if "A" in on:
                    pe.wait_ge(xhT_ready, i + 1)
                    project(ps_q[:, 256:512], xhT, wq_sb).then_inc(q_done, 1)
                if "B" in on:
                    turn(i - 1, 0)
                if "V" in on:
                    values(i - 2, p, 3)
                if "M" in on:
                    pe.wait_ge(xh2_ready, i - 2)
                    two_transposes(ps_c[:, 0:256], xh2[:, q]).then_inc(x2T_done, 1)
                if "B" in on:
                    scores(i - 1, q, 2)
                    turn(i - 1, 1)
                if "M" in on:
                    pe.wait_ge(xh2T_ready, i - 2)
                    project(ps_c[:, 256:256 + EXPERTS], xh2T, gate_sb).then_inc(router_done, 1)
                if "R" in on:
                    pe.wait_ge(taken_ready, i - 3)
                    mm(ps_c[:, RANK:RANK + EXPERTS], tri[:], taken[:])
                    mm(ps_c[:, RANK + EXPERTS:RANK + 2 * EXPERTS], ones_bf[:], taken[:]).then_inc(rank_done, 1)
                if "A" in on:
                    pe.wait_ge(v_ready, i + 1)
                    alone(pe)
                    pe.wait_ge(k_ready, i + 1)
                    alone(pe)
                    two_transposes(ps_kv, k_rot).then_inc(kT_done, 1)
                if "B" in on:
                    scores(i - 1, q, 3)
                    values(i - 1, q, 0)
                if "V" in on:
                    pe.wait_ge(attn_ready, i - 1)
                    reached(pe, expl_ready, i - 2)
                    two_transposes(ps_c[:, 0:256], attn).then_inc(aT_done, 1)
                if "A" in on:
                    pe.wait_ge(q_ready, i + 1)
                    alone(pe)
                    two_transposes(ps_q, q_rot).then_inc(qT_done, 1)
                if "B" in on:
                    turn(i - 1, 2)
                if "V" in on:
                    pe.wait_ge(attnT_ready, i - 1)
                    project(ps_c[:, 256:512], attnT, wo_sb).then_inc(wo_done, 1)
                if "B" in on:
                    values(i - 1, q, 1)
                if "L" in on:
                    turn_x(i + 1)
                if isinstance(i, int) and i == 1:
                    pe.wait_ge(later_in, 16 * 4)
                    pe.wait_ge(dve_const, 7)

            pe.wait_ge(const_in, 16)
            pe.wait_ge(consts_ready, 7)
            turn_x(0)
            pe.wait_ge(weights_in, 16 * 3)
            pipeline(pe, step)

            pe.wait_ge(gu_in, 16 * 8)
            pe.wait_ge(slot_ready, TILES)

            def turn_block(b, u, rnd):
                p = u % 2
                if u % BG == 0:
                    pe.wait_ge(xb_in[u // BG], (rnd + 1) * 16)
                reached(pe, xbT_ready, b - 1)
                two_transposes(pp_xT[p], xb[:, u // BG, u % BG]).then_inc(xbT_done, 1)

            def gate_up_block(b, u, rnd):
                p = u % 2
                e = pe.value_load(xb[0:1, u // BG, u % BG, COL_EXP:COL_EXP + 1].bitcast(I32), min_val=0, max_val=EXPERTS - 1)
                pe.wait_ge(xbT_ready, b + 1)
                reached(pe, hid_ready, b - 1)
                for c in range(2):
                    m = mm(pp_gu[p][:, 0:2 * INNER], xbT[:, p, c, :],
                           gu_sb[:, bass.ds(e, 1), c, :].rearrange("p e n -> p (e n)"), start=c == 0, stop=c == 1)
                m.then_inc(gu_done, 1)

            def turn_hidden(b, u, rnd):
                p = u % 2
                pe.wait_ge(hid_ready, b + 1)
                reached(pe, hidT_ready, b - 1)
                t.transpose(pp_hT[p][0:INNER, 0:P], hid[:, p, :], ident).then_inc(hT_done, 1)

            def down_block(b, u, rnd):
                j, p = u % NB, u % 2
                pe.wait_ge(hidT_ready, b + 1)
                pe.wait_ge(w2_in[j], (rnd * (ROUND // NB) + u // NB + 1) * 16)
                reached(pe, yb_ready, b - 1)
                mm(pp_y[p][:, 0:DIM], hidT[:, p, :], w2_sb[:, j, :]).then_inc(y_done, 1)

            beats2(pe, {0: turn_block, 1: gate_up_block, 2: turn_hidden, 3: down_block})



def beats2(eng, stages):
    U = ROUND

    def beat(rounds, u):
        for s in sorted(stages):
            if isinstance(rounds, int) and not 0 <= rounds * U + u - s < BLOCKS:
                continue
            stages[s](rounds * U + (u - s), (u - s) % U, rounds + (u - s) // U)

    for u in range(U):
        beat(0, u)
    with eng.Fori(1, BLOCKS // U) as rounds:
        for u in range(U):
            beat(rounds, u)
    for u in range(max(stages)):
        beat(BLOCKS // U, u)


CHAIN_FULL = 23


def kernel(x, ctx_1024, fside_BxSx2_0, L0_xattn_Wq, L0_xattn_Wkv, L0_xattn_Wout, L0_xattn_bout,
           L0_ffn_gate_weight, L0_ffn_gate_up_proj, L0_ffn_down_proj):
    import concourse.bacc as bacc
    from concourse.bass_utils import run_bass_kernel_spmd

    def lay(a):
        return np.ascontiguousarray(a)

    def chunks(w):
        return lay(np.asarray(w).reshape(2, P, -1).transpose(1, 0, 2))

    wkv = np.asarray(L0_xattn_Wkv)
    const = np.zeros((P, C_END), np.float32)
    const[:, C_ID:C_ID + P] = np.eye(P)
    const[:, C_HM:C_HM + HG] = (np.arange(P)[:, None] % SEQ) // HD == np.arange(HG)
    const[:, C_IOTA:C_IOTA + EXPERTS] = np.arange(EXPERTS)
    const[:, C_DEST:C_DEST + TOPK] = np.arange(P)[:, None] * TOPK + np.arange(TOPK)
    const[:, C_TRI:C_TRI + P] = np.arange(P)[:, None] < np.arange(P)
    blank = np.zeros((P, ROW), np.int32)
    blank[:, COL_DEST] = 1 << 20
    arrays = {
        "x": lay(np.asarray(x).reshape(TOKENS, DIM)),
        "ctxT": lay(np.asarray(ctx_1024).reshape(TOKENS, CTX).T),
        "pos": lay(np.asarray(fside_BxSx2_0).reshape(TOKENS, 2)),
        "wq": chunks(L0_xattn_Wq),
        "wk": lay(wkv[:, :DIM]),
        "wv": lay(wkv[:, DIM:].reshape(CTX, PAIRS, 2, HD).transpose(0, 2, 1, 3).reshape(CTX, 2, DIM // 2)),
        "wo": chunks(L0_xattn_Wout),
        "bout": lay(np.broadcast_to(np.asarray(L0_xattn_bout), (P, DIM))),
        "gate": chunks(np.asarray(L0_ffn_gate_weight).T),
        "gu": lay(np.asarray(L0_ffn_gate_up_proj).transpose(2, 0, 1).reshape(2, P, EXPERTS, 2 * INNER).transpose(1, 2, 0, 3)),
        "w2": lay(np.asarray(L0_ffn_down_proj).transpose(0, 2, 1)),
        "const": const,
        "blank": blank.view(np.float32),
    }
    nc = bacc.Bacc("TRN2", target_bir_lowering=False, num_devices=1)
    aps = [nc.dram_tensor(f"in_{n}", a.shape, mybir.dt.from_np(a.dtype), kind="ExternalInput").ap() for n, a in arrays.items()]
    out = nc.dram_tensor("out", [TOKENS, DIM], F32, kind="ExternalOutput").ap()
    build(nc, *aps, out)
    r = run_bass_kernel_spmd(nc, [{f"in_{n}": a for n, a in arrays.items()}], core_ids=[0])
    return r.results[0]["out"].reshape(BATCH, SEQ, DIM)
```
